# Optimizing a Trainium2 kernel written in Bass

```python
import numpy as np
import jax
import jax.numpy as jnp

def _softmax(x, axis=-1):
    return jax.nn.softmax(x, axis=axis)

def _gelu(x):
    return jax.nn.gelu(x, approximate=True)

def _silu(x):
    return jax.nn.silu(x)

def _sigmoid(x):
    return jax.nn.sigmoid(x)

def _layernorm(x, axis=-1, eps=1e-05):
    m = jnp.mean(x, axis=axis, keepdims=True)
    v = jnp.var(x, axis=axis, keepdims=True)
    return (x - m) / jnp.sqrt(v + eps)

def _scatter_add(tgt, idx, src, axis=0):
    return tgt.at[idx].add(src)

def _segment_sum(src, seg, n):
    return jax.ops.segment_sum(src, seg, n)
kernel_name = 'mk_seq_preln_d1_jaxref_r2_746ca2'

def setup_inputs(seed: int=0):
    np.random.seed(seed)
    _w = jnp.asarray

    def _L0_attn_setup():
        import jax, jax.numpy as jnp
        import numpy as np
        B, S, E, H = (2, 1024, 512, 16)
        HD = E // H
        LAMBDA_INIT = 0.8
        EPS = 1e-06
        key = jax.random.key(seed)
        ks = jax.random.split(key, 8)
        return {'x': jax.random.normal(ks[0], (B, S, E), dtype=jnp.float32), 'w_qkv': jax.random.normal(ks[1], (E, 3 * E), dtype=jnp.float32) * E ** (-0.5), 'wo': jax.random.normal(ks[2], (E, E), dtype=jnp.float32) * E ** (-0.5), 'lambda_q1': jax.random.normal(ks[3], (HD,), dtype=jnp.float32) * 0.1, 'lambda_q2': jax.random.normal(ks[4], (HD,), dtype=jnp.float32) * 0.1, 'lambda_k1': jax.random.normal(ks[5], (HD,), dtype=jnp.float32) * 0.1, 'lambda_k2': jax.random.normal(ks[6], (HD,), dtype=jnp.float32) * 0.1, 'norm_w': jnp.ones((H, HD), dtype=jnp.float32)}
    _L0_attn_in = _L0_attn_setup()

    def _L0_ffn_setup():
        import jax, jax.numpy as jnp
        import numpy as np

        def _bitlinear(x, w_latent):
            scale = jax.lax.stop_gradient(jnp.clip(jnp.mean(jnp.abs(w_latent), axis=1, keepdims=True), 1e-05, None))
            tern = jnp.clip(jnp.round(w_latent / scale), -1.0, 1.0)
            w = w_latent + jax.lax.stop_gradient(tern - w_latent)
            return x @ (w * scale).T
        key = jax.random.key(seed)
        ks = jax.random.split(key, 6)
        dim, hidden, rank = (512, 2048, 16)
        B, S = (4, 2048)
        x = jax.random.normal(ks[0], (B, S, dim), dtype=jnp.float32)
        w_fc = 0.02 * jax.random.normal(ks[1], (hidden, dim), dtype=jnp.float32)
        w_proj = 0.02 * jax.random.normal(ks[2], (dim, hidden), dtype=jnp.float32)
        u = 0.02 * jax.random.normal(ks[3], (hidden, rank), dtype=jnp.float32)
        v = 0.02 * jax.random.normal(ks[4], (rank, dim), dtype=jnp.float32)
        fast_b = jax.random.normal(ks[5], (rank, rank), dtype=jnp.float32)
        gate = jnp.float32(0.05)
        return {'x': x, 'fast_b': fast_b, 'w_fc': w_fc, 'w_proj': w_proj, 'u': u, 'v': v, 'gate': gate}
    _L0_ffn_in = _L0_ffn_setup()
    _d = {'L0_attn_x': _L0_attn_in['x'], 'L0_attn_w_qkv': _L0_attn_in['w_qkv'], 'L0_attn_wo': _L0_attn_in['wo'], 'L0_attn_lambda_q1': _L0_attn_in['lambda_q1'], 'L0_attn_lambda_q2': _L0_attn_in['lambda_q2'], 'L0_attn_lambda_k1': _L0_attn_in['lambda_k1'], 'L0_attn_lambda_k2': _L0_attn_in['lambda_k2'], 'L0_attn_norm_w': _L0_attn_in['norm_w'], 'L0_ffn_fast_b': _L0_ffn_in['fast_b'], 'L0_ffn_w_fc': _L0_ffn_in['w_fc'], 'L0_ffn_w_proj': _L0_ffn_in['w_proj'], 'L0_ffn_u': _L0_ffn_in['u'], 'L0_ffn_v': _L0_ffn_in['v'], 'L0_ffn_gate': _L0_ffn_in['gate']}
    _x0 = _d['L0_attn_x']
    _d['L0_attn_x'] = jax.random.normal(jax.random.fold_in(jax.random.key(seed), 1), (8, 1024, 512), dtype=_x0.dtype)
    del _x0
    return _d

def reference(L0_attn_x, L0_attn_w_qkv, L0_attn_wo, L0_attn_lambda_q1, L0_attn_lambda_q2, L0_attn_lambda_k1, L0_attn_lambda_k2, L0_attn_norm_w, L0_ffn_fast_b, L0_ffn_w_fc, L0_ffn_w_proj, L0_ffn_u, L0_ffn_v, L0_ffn_gate):

    def _L0_attn_ref(x, w_qkv, wo, lambda_q1, lambda_q2, lambda_k1, lambda_k2, norm_w):
        import jax, jax.numpy as jnp
        import numpy as np
        B, S, E, H = (2, 1024, 512, 16)
        HD = E // H
        LAMBDA_INIT = 0.8
        EPS = 1e-06
        b, s, e = x.shape
        qkv = x @ w_qkv
        q, k, v = jnp.split(qkv, 3, axis=-1)

        def to_heads(t):
            return t.reshape(b, s, H, HD).transpose(0, 2, 1, 3)
        q, k, v = (to_heads(q), to_heads(k), to_heads(v))
        q1, q2 = jnp.split(q, 2, axis=-1)
        k1, k2 = jnp.split(k, 2, axis=-1)
        scale = 1.0 / jnp.sqrt(jnp.asarray(HD, dtype=x.dtype))
        a1 = jax.nn.softmax(jnp.einsum('bhsd,bhtd->bhst', q1, k1) * scale, axis=-1)
        a2 = jax.nn.softmax(jnp.einsum('bhsd,bhtd->bhst', q2, k2) * scale, axis=-1)
        lam = jnp.exp(jnp.dot(lambda_q1, lambda_k1)) - jnp.exp(jnp.dot(lambda_q2, lambda_k2)) + LAMBDA_INIT
        a = a1 - lam * a2
        out = jnp.einsum('bhst,bhtd->bhsd', a, v)
        rms = jnp.sqrt(jnp.mean(out * out, axis=-1, keepdims=True) + EPS)
        out_n = out / rms * norm_w[None, :, None, :] * (1.0 - LAMBDA_INIT)
        out_cat = out_n.reshape(b, H * s, HD)
        out_final = out_cat.transpose(0, 2, 1).reshape(b, s, e)
        return out_final @ wo

    def _L0_ffn_ref(x, fast_b, w_fc, w_proj, u, v, gate):
        import jax, jax.numpy as jnp
        import numpy as np

        def _bitlinear(x, w_latent):
            scale = jax.lax.stop_gradient(jnp.clip(jnp.mean(jnp.abs(w_latent), axis=1, keepdims=True), 1e-05, None))
            tern = jnp.clip(jnp.round(w_latent / scale), -1.0, 1.0)
            w = w_latent + jax.lax.stop_gradient(tern - w_latent)
            return x @ (w * scale).T
        h = _bitlinear(x, w_fc) + gate * (x @ v.T @ fast_b.T @ u.T)
        r = jnp.maximum(h, 0.0)
        return _bitlinear(r * r, w_proj)
    x = L0_attn_x
    x = x + _L0_attn_ref(_layernorm(x, axis=-1), L0_attn_w_qkv, L0_attn_wo, L0_attn_lambda_q1, L0_attn_lambda_q2, L0_attn_lambda_k1, L0_attn_lambda_k2, L0_attn_norm_w)
    x = x + _L0_ffn_ref(_layernorm(x, axis=-1), L0_ffn_fast_b, L0_ffn_w_fc, L0_ffn_w_proj, L0_ffn_u, L0_ffn_v, L0_ffn_gate)
    return x

_drawn_inputs = setup_inputs


def setup_inputs(seed=0):
    import zlib

    import numpy as np

    out = dict(_drawn_inputs(seed))
    spreads = {'L0_attn_norm_w': (1.0, 0.2)}
    factors = {'L0_attn_lambda_q1': 2.892,
     'L0_attn_lambda_k1': 5.667,
     'L0_attn_lambda_k2': 3.179,
     'L0_ffn_fast_b': 8.0,
     'L0_ffn_u': 8.0,
     'L0_ffn_v': 8.0}
    for name, (base, spread) in spreads.items():
        noise = np.random.default_rng([zlib.crc32(name.encode()), seed]).standard_normal(out[name].shape)
        drawn = base * np.exp(spread * noise) if base else spread * noise
        out[name] = jnp.asarray(drawn.astype(out[name].dtype))
    for name, factor in factors.items():
        out[name] = (out[name] * factor).astype(out[name].dtype)
    return out
```

```python
import numpy as np
import concourse.bass as bass
from concourse import mybir
from contextlib import ExitStack

F32 = mybir.dt.float32
FR = mybir.dt.float32r
BF16 = mybir.dt.bfloat16
I32 = mybir.dt.int32
ALU = mybir.AluOpType
ACT = mybir.ActivationFunctionType
AX = mybir.AxisListType

B, S, E, H, HD = 8, 1024, 512, 16, 32
HID, RANK = 2048, 16
NP = H // 2
SCALE = float(1.0 / np.sqrt(np.float32(HD)))
LAMBDA_INIT = 0.8
RING = 3
NPB = 3
SAFE = 32.0


class Queues:

    ENGINES = ("tensor", "scalar", "vector", "gpsimd", "sync")

    def __init__(self, nc, ctx):
        self.nc, self.ctx = nc, ctx
        self.items = {e: [] for e in self.ENGINES}
        self.value = {}
        self.done = {e: self.sem("s_" + e) for e in self.ENGINES[:4]}

    def sem(self, name):
        s = self.ctx.enter_context(self.nc.semaphore(name))
        self.value[name] = 0
        return (name, s)

    def op(self, engine, fn, waits=(), tok=False):
        sem = self.done[engine] if tok else None
        self.items[engine].append((fn, [w for w in waits if w is not None], sem, 1))
        if tok:
            self.value[sem[0]] += 1
            return (sem, self.value[sem[0]])
        return None

    def dma(self, engine, sem, dst, src, waits=(), **how):
        self.items[engine].append((lambda e: e.dma_start(dst, src, **how), [w for w in waits if w is not None], sem, 16))
        self.value[sem[0]] += 16
        return (sem, self.value[sem[0]])

    def expect(self, sem, n):
        self.value[sem[0]] += n
        return (sem, self.value[sem[0]])

    def fence(self, extra=()):
        toks = [self.op(e, lambda eng: eng.drain(), tok=True) for e in self.ENGINES[:4]]
        for e in self.ENGINES:
            self.op(e, None, toks + list(extra))

    def play(self, block):
        at = {"tensor": block.tensor, "scalar": block.scalar, "vector": block.vector, "gpsimd": block.gpsimd,
              "sync": block.sync}

        def body(name):
            def run(eng):
                seen = {}
                for fn, waits, sem, inc in self.items[name]:
                    for (wname, wsem), v in waits:
                        if seen.get(wname, 0) < v:
                            eng.wait_ge(wsem, v)
                            seen[wname] = v
                    if fn is None:
                        continue
                    ins = fn(eng)
                    if sem is not None:
                        ins.then_inc(sem[1], inc)
            at[name](run)
        for name in self.ENGINES:
            body(name)


def build(nc, x, wqkv, wo, lq1, lq2, lk1, lk2, norm_w, fast_b, w_fc, w_proj, u, v, gate, out):
    x2d = nc.dram_tensor("x2_scratch", [B * S, E], F32, kind="Internal").ap()
    qsc = nc.dram_tensor("q_scratch", [2, 4, 8, 3, 16, S], BF16, kind="Internal").ap()
    ksc = nc.dram_tensor("k_scratch", [2, 4, 8, 3, 16, S], BF16, kind="Internal").ap()

    with ExitStack() as top:
        Q = Queues(nc, top)
        op, dma = Q.op, Q.dma
        ps = top.enter_context(nc.psum_tensor("ps", [128, 8, 512], F32))

        def sbuf(ctx, name, shape, dt=F32):
            return ctx.enter_context(nc.sbuf_tensor(name, shape, dt))

        ident = sbuf(top, "ident", [128, 128])
        small = sbuf(top, "small", [128, 64])
        ind = sbuf(top, "ind", [128, 8])
        eps5, eps6, neglam, gatec = small[:, 0:1], small[:, 1:2], small[:, 2:3], small[:, 3:4]

        op("scalar", lambda e: (e.preload_act_table_set("natural_log_exp_and_others"), None)[1])
        t_c0 = [op("gpsimd", lambda e: e.memset(ident[:], 0.0), tok=True),
                op("gpsimd", lambda e: e.memset(ind[:], 1.0), tok=True)]
        t_ident = op("gpsimd", lambda e: e.affine_select(out=ident[:], in_=ident[:], compare_op=ALU.not_equal, fill=1.0,
                     base=0, pattern=[[-1, 128]], channel_multiplier=1), [t_c0[0]], tok=True)
        t_i1 = op("gpsimd", lambda e: e.affine_select(out=ind[:], in_=ind[:], compare_op=ALU.is_ge, fill=0.0,
                  base=0, pattern=[[-16, 8]], channel_multiplier=1), [t_c0[1]], tok=True)
        t_ind = op("gpsimd", lambda e: e.affine_select(out=ind[:], in_=ind[:], compare_op=ALU.is_ge, fill=0.0,
                   base=15, pattern=[[16, 8]], channel_multiplier=-1), [t_i1], tok=True)
        t_eps = [op("gpsimd", lambda e: e.memset(eps5, 1e-5), tok=True),
                 op("gpsimd", lambda e: e.memset(eps6, 1e-6), tok=True)]
        s_small = Q.sem("s_small")
        t_gate = dma("sync", s_small, gatec, gate.partition_broadcast(128))

        ln_prev = []

        def layernorm(xin, xout, mv, st6, rs, ln_t, n, waits, wout=()):
            t = []
            for i in range(n):
                t.append(op("vector", lambda e, i=i: e.bn_stats(st6[:, i, :], xin[:, i, :]), [*waits, *ln_prev], tok=True))
            for i in range(n):
                a = op("vector", lambda e, i=i: e.bn_aggr(mv[:, i, :], st6[:, i, :]), [t[i]], tok=True)
            var = mv[:, 0:n, 1]
            l1 = op("scalar", lambda e: e.activation(ln_t[:, 0:n], var, ACT.Ln, bias=eps5), [a] + t_eps, tok=True)
            l2 = op("scalar", lambda e: e.activation(rs[:, 0:n], ln_t[:, 0:n], ACT.Exp, scale=-0.5), [l1], tok=True)
            h = ln_t[:, 8:8 + n]
            g = ln_t[:, 16:16 + n]
            c1 = op("vector", lambda e: e.tensor_tensor(h, rs[:, 0:n], rs[:, 0:n], ALU.mult), [l2], tok=True)
            c2 = op("vector", lambda e: e.tensor_scalar(g, var, 1e-5, -0.5, ALU.add, ALU.mult), [a], tok=True)
            c3 = op("vector", lambda e: e.tensor_tensor(h, h, g, ALU.mult), [c1, c2], tok=True)
            c4 = op("vector", lambda e: e.scalar_tensor_tensor(out=rs[:, 8:8 + n], in0=h, scalar=1.5, in1=rs[:, 0:n],
                    op0=ALU.add, op1=ALU.mult), [c3], tok=True)
            for i in range(n):
                last = op("vector", lambda e, i=i: e.tensor_scalar(xout[:, i, :], xin[:, i, :], mv[:, i, 0:1],
                          rs[:, 8 + i:9 + i], ALU.subtract, ALU.mult), [c4, *wout], tok=True)
            ln_prev[:] = [last]
            return last

        with ExitStack() as g1:
            wqh = sbuf(g1, "wqh", [128, 4, 3 * E], FR)
            wql = sbuf(g1, "wql", [128, 4, 3 * E], FR)
            woh = sbuf(g1, "woh", [128, 4, E], FR)
            wol = sbuf(g1, "wol", [128, 4, E], FR)
            qst = sbuf(g1, "qst", [128, RING, 4, S], BF16)
            kst = sbuf(g1, "kst", [128, RING, 4, S], BF16)
            vt = sbuf(g1, "vt", [128, 8, E])
            acc = sbuf(g1, "acc", [128, 2, 2 * S])
            xin = sbuf(g1, "xin", [128, 4, E])
            lnt = sbuf(g1, "lnt", [128, E])
            rl = sbuf(g1, "rl", [128, 2, E])
            t1 = sbuf(g1, "t1", [128, E])
            ot = sbuf(g1, "ot", [128, E])
            sq = sbuf(g1, "sq", [128, E])
            rr = sbuf(g1, "rr", [128, E])
            on = sbuf(g1, "on", [128, E])
            oth = sbuf(g1, "oth", [128, 4, 128], FR)
            otl = sbuf(g1, "otl", [128, 4, 128], FR)
            xr = sbuf(g1, "xr", [128, E])
            sqb = sbuf(g1, "sqb", [128, 2, E], BF16)
            indb = sbuf(g1, "indb", [128, 8], BF16)
            blk = sbuf(g1, "blk", [128, 128])
            ones = sbuf(g1, "ones", [128, 32])
            nw = sbuf(g1, "nw", [128, NP])
            mx = sbuf(g1, "mx", [128, 128])
            mh = sbuf(g1, "mh", [32, 3, 128], BF16)
            mr = sbuf(g1, "mr", [32, 128])
            mv = sbuf(g1, "mv", [128, 4, 2])
            st6 = sbuf(g1, "st6", [128, 4, 6])
            rs = sbuf(g1, "rs", [128, 16])
            ln_t = sbuf(g1, "ln_t", [128, 24])
            nmx = sbuf(g1, "nmx", [8, 40])
            fl = sbuf(g1, "fl", [1, 1], I32)
            lam = sbuf(g1, "lam", [128, 4, HD])
            with ExitStack() as al:
                pr = sbuf(al, "pr", [128, NPB, 2, S])
            with ExitStack() as al:
                xth = sbuf(al, "xth", [128, 4, 512], FR)
                xtl = sbuf(al, "xtl", [128, 4, 512], FR)
                hml = sbuf(al, "hml", [128, 2, 3, 512], BF16)
                r1 = sbuf(al, "r1", [128, 512])
            with ExitStack() as al:
                wst = sbuf(al, "wst", [128, 4, 3 * E])

            s_w = Q.sem("s_w")
            s_wo = Q.sem("s_wo")
            s_x = Q.sem("s_x")
            s_hml = [Q.sem("s_hml0"), Q.sem("s_hml1")]
            s_ring = [Q.sem(f"s_ring{i}") for i in range(RING)]
            s_mh = Q.sem("s_mh")
            s_xr = Q.sem("s_xr")
            s_x2 = Q.sem("s_x2")
            s_gpe = Q.sem("s_gpe")
            s_gdve = Q.sem("s_gdve")

            t_w = dma("sync", s_w, wst[:], wqkv.rearrange("(k p) n -> p k n", p=128))
            x_chunk = lambda b, c: x[b, c * 512:(c + 1) * 512, :].rearrange("(t p) e -> p t e", p=128)
            t_x = dma("sync", s_x, xin[:], x_chunk(0, 0))
            for i, l in enumerate((lq1, lk1, lq2, lk2)):
                t_lam = dma("sync", s_small, lam[:, i, :], l.partition_broadcast(128))
            nwr = norm_w.rearrange("(p h) d -> h d p", h=2)
            for i in range(4):
                t_nw = dma("sync", s_small, nw[32 * i:32 * i + 32, :], nwr[i // 2], allow_slow_non_contiguous=True)
            t_wh = op("scalar", lambda e: e.activation(wqh[:], wst[:], ACT.Copy), [t_w], tok=True)
            t_wl = op("vector", lambda e: e.tensor_tensor(wql[:], wst[:], wqh[:], ALU.subtract), [t_wh], tok=True)
            t_w2 = dma("sync", s_wo, wst[:, :, 0:E], wo.rearrange("(k p) n -> p k n", p=128), [t_wl, t_wh])
            t_woh = op("scalar", lambda e: e.activation(woh[:], wst[:, :, 0:E], ACT.Copy), [t_w2], tok=True)
            t_wol = op("vector", lambda e: e.tensor_tensor(wol[:], wst[:, :, 0:E], woh[:], ALU.subtract), [t_woh], tok=True)
            dt_ = small[:, 8:16]
            tl = [op("vector", lambda e, i=i: e.tensor_tensor(lam[:, 2 * i, :], lam[:, 2 * i, :], lam[:, 2 * i + 1, :],
                     ALU.mult), [t_nw], tok=True) for i in range(2)]
            tl = [op("vector", lambda e, i=i: e.tensor_reduce(dt_[:, i:i + 1], lam[:, 2 * i, :], AX.X, ALU.add),
                     [tl[i]], tok=True) for i in range(2)]
            t_le = op("scalar", lambda e: e.activation(dt_[:, 2:4], dt_[:, 0:2], ACT.Exp), tl, tok=True)
            t_ld = op("vector", lambda e: e.tensor_tensor(dt_[:, 4:5], dt_[:, 3:4], dt_[:, 2:3], ALU.subtract), [t_le], tok=True)
            t_lam = op("vector", lambda e: e.tensor_scalar(neglam, dt_[:, 4:5], -LAMBDA_INIT, None, ALU.add), [t_ld], tok=True)
            t_nw = op("vector", lambda e: e.tensor_scalar(nw[:], nw[:], 1.0 - LAMBDA_INIT, None, ALU.mult), [t_nw], tok=True)
            t_indb = op("vector", lambda e: e.tensor_copy(indb[:], ind[:]), [t_ind], tok=True)
            tc = [op("vector", lambda e: e.memset(blk[:], 0.0), tok=True),
                  op("vector", lambda e: e.memset(ones[:], 1.0), tok=True),
                  op("vector", lambda e: e.memset(mx[:], 0.0), tok=True),
                  op("vector", lambda e: e.memset(kst[96:128, :, :, :], 1.0), tok=True)]
            for i in range(4):
                t_blk = op("vector", lambda e, i=i: e.memset(blk[32 * i:32 * i + 32, 32 * i:32 * i + 32], 1.0), [tc[0]], tok=True)
            t_ones = tc[3]

            bank = {i: [] for i in range(8)}
            p_free = [[t_wol, t_woh] for _ in range(NPB)]
            d1_free = [t_wol, t_woh]
            acc_free = [[], []]
            ring_free = [[] for _ in range(RING)]
            hml_free = [[], []]
            vt_free = []
            mh_free = []
            r_free = [[], []]
            xr_free = []
            lnt_free = []
            rr_free = []
            sq_free = []
            ot_free = []
            ot_w = []
            r1_free = []
            t1_free = []
            on_free = []
            ott_free = []
            sqb_free = [[], []]
            xin_free = []
            events = {}
            slot = [0]

            def at(delay, fn):
                events.setdefault(slot[0] + delay, []).append(fn)

            def tick():
                for fn in events.pop(slot[0], []):
                    fn()
                slot[0] += 1

            reg = {}

            def transpose_chunk(t_ln):
                for k in range(4):
                    bk = k
                    for st in range(4):
                        t = op("tensor", lambda e, k=k, st=st, bk=bk: e.transpose(
                            ps[:, bk, st * 128:(st + 1) * 128], xin[:, st, k * 128:(k + 1) * 128], ident[:]),
                            [t_ln, t_ident, *bank[bk]], tok=(st == 3))
                    a = op("scalar", lambda e, k=k, bk=bk: e.activation(xth[:, k, :], ps[:, bk, :], ACT.Copy),
                           [t, *d1_free], tok=True)
                    d = op("vector", lambda e, k=k, bk=bk: e.tensor_tensor(xtl[:, k, :], ps[:, bk, :], xth[:, k, :],
                           ALU.subtract), [a, *d1_free], tok=True)
                    bank[bk] = [a, d]
                xin_free[:] = [t]
                return d

            def project(dst, mcol, lhs, waits):
                n = 0
                for k in range(4):
                    for w, xx in ((wqh, xth), (wql, xth), (wqh, xtl)):
                        if lhs == "w":
                            f = lambda e, k=k, w=w, xx=xx, n=n: e.matmul(
                                dst, w[:, k, mcol:mcol + 128], xx[:, k, :], start=(n == 0), stop=(n == 11))
                        else:
                            f = lambda e, k=k, w=w, xx=xx, n=n: e.matmul(
                                dst, xx[:, k, lhs * 128:(lhs + 1) * 128], w[:, k, mcol:mcol + 512],
                                start=(n == 0), stop=(n == 11))
                        t = op("tensor", f, waits, tok=(n == 11))
                        n += 1
                return t

            mcount = [0]
            vcount = [0]

            def qk_tile(b, c, m, t_xt):
                i = mcount[0]
                mcount[0] += 1
                bk = i % 4
                t = project(ps[:, bk, :], m * 128, "w", [t_xt, t_wl, *bank[bk]])
                hb = i % 2
                p = ps[:, bk, :]
                h_, m_, l_ = (hml[:, hb, j, :] for j in range(3))
                a = op("scalar", lambda e: e.activation(h_, p, ACT.Copy), [t, *hml_free[hb], *d1_free], tok=True)
                d1 = op("vector", lambda e: e.tensor_tensor(r1[:], p, h_, ALU.subtract), [a, *d1_free, *r1_free], tok=True)
                d2 = op("vector", lambda e: e.tensor_copy(m_, r1[:]), [d1], tok=True)
                d3 = op("vector", lambda e: e.tensor_tensor(l_, r1[:], m_, ALU.subtract), [d2], tok=True)
                bank[bk] = [a, d1]
                r1_free[:] = [d3]
                g = op("gpsimd", lambda e: e.tensor_tensor(sqb[:, hb, :], h_, h_, ALU.mult), [a, *sqb_free[hb]], tok=True)
                sc = (qsc if m < 4 else ksc)[b % 2, m % 4]
                order = (0, 1, 2) if m < 4 else (2, 1, 0)
                for cc, part in enumerate(order):
                    td = dma("sync", s_hml[hb], sc[:, cc, :, c * 512:(c + 1) * 512], hml[:, hb, part, :], [a, d3])
                hml_free[hb] = [td, g]
                nb = 4

                def norms():
                    tn = op("tensor", lambda e: e.matmul(ps[0:8, nb, :], indb[:], sqb[:, hb, :], start=True, stop=True),
                            [g, t_indb, *bank[nb]], tok=True)
                    dn = op("vector", lambda e: e.tensor_reduce(nmx[0:8, c * 8 + m:c * 8 + m + 1], ps[0:8, nb, :], AX.X,
                            ALU.max), [tn], tok=True)
                    bank[nb] = [dn]
                    sqb_free[hb] = [tn]
                    return dn
                return norms, td

            def v_tile(c, st, t_xt):
                i = mcount[0]
                mcount[0] += 1
                bk = i % 4
                t = project(ps[:, bk, :], 2 * E, st, [t_xt, t_wl, *bank[bk]])
                a = op("scalar", lambda e: e.activation(vt[:, c * 4 + st, :], ps[:, bk, :], ACT.Copy),
                       [t, *vt_free], tok=True)
                bank[bk] = [a]
                return t, a

            def flag(t_n):
                a = op("vector", lambda e: e.tensor_tensor(nmx[:, 16:24], nmx[:, 0:8], nmx[:, 8:16], ALU.max), [t_n], tok=True)
                a = op("vector", lambda e: e.tensor_tensor(nmx[:, 24:28], nmx[:, 16:20], nmx[:, 20:24], ALU.mult), [a], tok=True)
                a = op("vector", lambda e: e.tensor_scalar(nmx[:, 28:32], nmx[:, 24:28], (SAFE / SCALE) ** 2, None,
                       ALU.is_gt), [a], tok=True)
                a = op("vector", lambda e: e.tensor_reduce(nmx[:, 32:33], nmx[:, 28:32], AX.X, ALU.max), [a], tok=True)
                t = op("tensor", lambda e: e.matmul(ps[0:1, 4, 0:1], nmx[0:8, 32:33], ones[0:8, 0:1], start=True, stop=True),
                       [a, t_ones, *bank[4]], tok=True)
                d = op("vector", lambda e: e.tensor_copy(fl[:], ps[0:1, 4, 0:1]), [t], tok=True)
                bank[4] = [d]
                z = op("vector", lambda e: e.memset(mh[:], 0.0), mh_free, tok=True)
                mh_free.clear()

                def load(name):
                    def fn(e):
                        reg[name] = e.value_load(fl[0:1, 0:1], min_val=0, max_val=8)
                    return fn
                op("tensor", load("tensor"), [d])
                op("vector", load("vector"), [d])
                return z

            def load_pair(b, q, t_sc):
                r = (b * NP + q) % RING
                tile, s0 = q // 2, 4 * (q % 2)
                w = [*t_sc, *ring_free[r]]
                row = 0
                for n in (3, 2, 1):
                    for dst, sc, c0 in ((qst, qsc, 0), (kst, ksc, 3 - n)):
                        t = dma("sync", s_ring[r], dst[row:row + 16 * n, r, :, :],
                                sc[b % 2, tile, s0:s0 + 4, c0:c0 + n].rearrange("s c d n -> (c d) s n"), w)
                    row += 16 * n
                return t

            def shift_pair(b, q, t_zero, t_stack, t_act):
                r = (b * NP + q) % RING
                base_pe, base_dve = Q.value["s_gpe"], Q.value["s_gdve"]
                spe, sdve = s_gpe[1], s_gdve[1]
                n_pe, n_dve = 33, 36
                prev_mh = list(mh_free)
                before = [*t_act, t_stack] + [w for bk in range(4) for w in bank[bk]]

                def pe(e):
                    with e.If(reg["tensor"] > 0):
                        for (_, ws), v_ in before:
                            e.wait_ge(ws, v_)
                        for i in range(32):
                            sl, st = i // 8, i % 8
                            if i >= 2:
                                e.wait_ge(sdve, base_dve + i - 1)
                            for c in range(2):
                                l = e.matmul(ps[:, 2 * (i % 2) + c, :], qst[0:96, r, sl, st * 128:(st + 1) * 128],
                                             kst[0:96, r, sl, c * 512:(c + 1) * 512], start=True, stop=True)
                            l.then_inc(spe, 1)
                        e.wait_ge(sdve, base_dve + 32)
                        e.transpose(ps[:, 0, 0:128], mx[:], ident[:]).then_inc(spe, 1)
                        e.wait_ge(sdve, base_dve + n_dve)
                    with e.Else():
                        e.sem_inc(spe, n_pe)

                def dve(e):
                    with e.If(reg["vector"] > 0):
                        for (_, ws), v_ in prev_mh:
                            e.wait_ge(ws, v_)
                        for i in range(32):
                            e.wait_ge(spe, base_pe + i + 1)
                            e.tensor_reduce(mx[:, i:i + 1], ps[:, 2 * (i % 2):2 * (i % 2) + 2, :], AX.XY, ALU.max)\
                                .then_inc(sdve, 1)
                        e.wait_ge(spe, base_pe + 33)
                        e.tensor_scalar(mh[:, 0, :], ps[0:32, 0, 0:128], -1.0, None, ALU.mult).then_inc(sdve, 1)
                        e.wait_ge(sdve, base_dve + 33)
                        e.scalar_tensor_tensor(out=mr[:], in0=ps[0:32, 0, 0:128], scalar=-1.0, in1=mh[:, 0, :],
                                               op0=ALU.mult, op1=ALU.subtract).then_inc(sdve, 1)
                        e.wait_ge(sdve, base_dve + 34)
                        e.tensor_copy(mh[:, 1, :], mr[:]).then_inc(sdve, 1)
                        e.wait_ge(sdve, base_dve + 35)
                        e.tensor_tensor(mh[:, 2, :], mr[:], mh[:, 1, :], ALU.subtract).then_inc(sdve, 1)
                    with e.Else():
                        e.sem_inc(sdve, n_dve)

                op("tensor", pe)
                op("vector", dve)
                Q.expect(s_gpe, n_pe)
                t_m = Q.expect(s_gdve, n_dve)
                for c in range(3):
                    t = dma("sync", s_ring[r], qst[96 + c:97 + c, r, :, :].rearrange("o s (t i) -> o (s t) i", i=128),
                            mh[:, c, :], [t_m, t_zero, *ring_free[r]])
                mh_free[:] = [t]
                return t

            def post_half(b, p, j, t_pv, t_acc):
                st = {}
                a0 = 6 + j

                def p_l():
                    for c4 in range(4):
                        t = op("tensor", lambda e, c4=c4: e.matmul(ps[32 * c4:32 * c4 + 32, a0, :], ones[:],
                               acc[:, j, c4 * 512:(c4 + 1) * 512], start=True, stop=True),
                               [t_acc, t_ones, *bank[a0]], tok=(c4 == 3))
                    st["l"] = t
                    acc_free[j] = [t]

                def p_r():
                    a = op("scalar", lambda e: e.activation(lnt[:], ps[:, a0, :], ACT.Ln), [st["l"], *lnt_free], tok=True)
                    bank[a0] = [a]
                    a = op("scalar", lambda e: e.activation(rl[:, j, :], lnt[:], ACT.Exp, scale=-1.0),
                           [a, *r_free[j]], tok=True)
                    lnt_free[:] = [a]
                    st["r"] = a

                def p_t():
                    if j == 0:
                        t = op("vector", lambda e: e.tensor_tensor(t1[:], ps[:, 4, :], rl[:, 0, :], ALU.mult),
                               [t_pv, st["r"], *t1_free], tok=True)
                        bank[4] = [t]
                        r_free[0] = [t]
                        ot_w[:] = [t]
                        return
                    t = op("vector", lambda e: e.scalar_tensor_tensor(out=ot[:], in0=ps[:, 5, :], scalar=neglam,
                           in1=rl[:, 1, :], op0=ALU.mult, op1=ALU.mult), [t_pv, st["r"], t_lam, *ot_free], tok=True)
                    bank[5] = [t]
                    r_free[1] = [t]
                    t = op("vector", lambda e: e.tensor_tensor(ot[:], ot[:], t1[:], ALU.add), [t, *ot_w], tok=True)
                    t1_free[:] = [t]
                    st["o"] = t
                    st["s"] = op("gpsimd", lambda e: e.tensor_tensor(sq[:], ot[:], ot[:], ALU.mult), [t, *sq_free], tok=True)

                def p_rms():
                    t = op("tensor", lambda e: e.matmul(ps[:, 6, :], blk[:], sq[:], start=True, stop=True),
                           [st["s"], t_blk, *bank[6]], tok=True)
                    sq_free[:] = [t]
                    st["m"] = t

                def p_rr():
                    a = op("scalar", lambda e: e.activation(lnt[:], ps[:, 6, :], ACT.Ln, bias=eps6, scale=1.0 / HD),
                           [st["m"], *lnt_free, *t_eps], tok=True)
                    bank[6] = [a]
                    a = op("scalar", lambda e: e.activation(rr[:], lnt[:], ACT.Exp, scale=-0.5), [a, *rr_free], tok=True)
                    lnt_free[:] = [a]
                    st["rr"] = a

                def p_on():
                    t = op("vector", lambda e: e.scalar_tensor_tensor(out=on[:], in0=ot[:], scalar=nw[:, p:p + 1], in1=rr[:],
                           op0=ALU.mult, op1=ALU.mult), [st["rr"], st["o"], t_nw, *on_free], tok=True)
                    rr_free[:] = [t]
                    ot_free[:] = [t, st["s"]]
                    st["on"] = t

                def p_tr():
                    for k in range(4):
                        t = op("tensor", lambda e, k=k: e.transpose(ps[:, 7, k * 128:(k + 1) * 128],
                               on[:, k * 128:(k + 1) * 128], ident[:]), [st["on"], *bank[7]], tok=(k == 3))
                    on_free[:] = [t]
                    st["tr"] = t

                def p_hl():
                    src = ps[:, 7, :].rearrange("p (k n) -> p k n", k=4)
                    a = op("scalar", lambda e: e.activation(oth[:], src, ACT.Copy), [st["tr"], *ott_free], tok=True)
                    d = op("vector", lambda e: e.tensor_tensor(otl[:], src, oth[:], ALU.subtract), [a, *ott_free], tok=True)
                    bank[7] = [a, d]
                    st["hl"] = d

                def p_wo():
                    n = 0
                    for k in range(4):
                        for o_, w_ in ((oth, woh), (oth, wol), (otl, woh)):
                            t = op("tensor", lambda e, k=k, o_=o_, w_=w_, n=n: e.matmul(
                                ps[:, 6, :], o_[:, k, :], w_[:, k, :], start=(n == 0), stop=(n == 11)),
                                [st["hl"], t_wol, *bank[6]], tok=(n == 11))
                            n += 1
                    ott_free[:] = [t]
                    st["wo"] = t

                def p_x2():
                    rows = x2d[b * S:(b + 1) * S, :].rearrange("(d g) e -> g d e", g=32)[4 * p:4 * p + 4]
                    d = op("vector", lambda e: e.tensor_tensor(xr[:], ps[:, 6, :], xr[:], ALU.add),
                           [st["wo"], st["xr"]], tok=True)
                    bank[6] = [d]
                    t = dma("sync", s_x2, rows, xr[:], [d])
                    xr_free[:] = [t]

                def p_ld():
                    st["xr"] = dma("sync", s_xr, xr[:], x[b].rearrange("(d g) e -> g d e", g=32)[4 * p:4 * p + 4], xr_free)

                at(2, p_l)
                at(3, p_r)
                at(4, p_t)
                if j == 1:
                    at(2, p_ld)
                    at(6, p_rms)
                    at(7, p_rr)
                    at(8, p_on)
                    at(9, p_tr)
                    at(10, p_hl)
                    at(12, p_wo)
                    at(13, p_x2)

            ln_tok = {}

            def prefetch_x(b, c):
                ln_tok["x"] = dma("sync", s_x, xin[:], x_chunk(b, c), xin_free)

            def prefetch_ln(b, c):
                ln_tok["ln"] = layernorm(xin, xin, mv, st6, rs, ln_t, 4, [ln_tok["x"]])

            ln_tok["x"] = t_x
            prefetch_ln(0, 0)
            for b in range(B):
                t_sc = {}
                pend = []
                t_n = None
                for c in range(2):
                    if c == 1:
                        prefetch_ln(b, 1)
                    t_xt = transpose_chunk(ln_tok["ln"])
                    if c == 0:
                        prefetch_x(b, 1)
                    for m in (0, 4, 1, 5, 2, 6, 3, 7):
                        nrm, td = qk_tile(b, c, m, t_xt)
                        t_sc[m] = td
                        if pend:
                            t_n = pend.pop()()
                        pend.append(nrm)
                        tick()
                    t_n = pend.pop()()
                    if c == 1:
                        t_zero = flag(t_n)
                        all_sc = list(t_sc.values())
                        tl_ = {q: load_pair(b, q, all_sc) for q in range(RING)}
                    for st in range(4):
                        t_vp, t_va = v_tile(c, st, t_xt)
                        tick()
                    d1_free = [t_vp]
                d1_end = [t_vp, *hml_free[0], *hml_free[1]]
                for s in range(NPB):
                    p_free[s] = list(d1_end)
                exp_tok = {}
                s_tok = [None, None]
                last_pv = [None]
                t_ring = {0: shift_pair(b, 0, t_zero, tl_[0], [])}
                if b + 1 < B:
                    prefetch_x(b + 1, 0)
                add_tok = [None]

                def pv(g):
                    q, j, t = g // 16, (g // 8) % 2, g % 8
                    sl = g % NPB
                    for c4 in range(4):
                        hh, ch = c4 // 2, c4 % 2
                        col = (2 * q + hh) * HD
                        tk = op("tensor", lambda e, c4=c4, hh=hh, ch=ch, col=col, t=t, j=j, sl=sl: e.matmul(
                            ps[32 * c4:32 * c4 + 32, 4 + j, :], vt[:, t, col:col + HD],
                            pr[:, sl, hh, ch * 512:(ch + 1) * 512], start=(t == 0), stop=(t == 7)),
                            [exp_tok[g], t_va] + (bank[4 + j] if t == 0 else []), tok=(c4 == 3))
                    last_pv[0] = tk
                    p_free[sl].append(tk)
                    if t == 7:
                        post_half(b, q, j, tk, add_tok[0])

                for g in range(16 * NP):
                    q, j, t = g // 16, (g // 8) % 2, g % 8
                    r = (b * NP + q) % RING
                    sl = g % NPB

                    def score(hh, r=r, j=j, t=t):
                        w = [t_ring[q], *(bank[2 * hh] + bank[2 * hh + 1])]
                        for c in range(2):
                            tk = op("tensor", lambda e, c=c: e.matmul(
                                ps[:, 2 * hh + c, :], kst[0:99, r, 2 * hh + j, t * 128:(t + 1) * 128],
                                qst[0:99, r, 2 * hh + j, c * 512:(c + 1) * 512], start=True, stop=True), w, tok=(c == 1))
                        return tk

                    def expo(hh, tk, sl=sl):
                        a = op("scalar", lambda e: e.activation(pr[:, sl, hh, :].rearrange("p (c n) -> p c n", c=2),
                               ps[:, 2 * hh:2 * hh + 2, :], ACT.Exp, scale=SCALE), [tk, *p_free[sl]], tok=True)
                        bank[2 * hh] = [a]
                        bank[2 * hh + 1] = [a]
                        return a

                    t0 = score(0)
                    if g:
                        pv(g - 1)
                    tS = score(1)
                    expo(0, t0)
                    exp_tok[g] = expo(1, tS)
                    p_free[sl] = []
                    if t == 1:
                        d = op("vector", lambda e, j=j, s0=(g - 1) % NPB, s1=sl: e.tensor_tensor(
                            acc[:, j, :], pr[:, s0, :, :].rearrange("p a n -> p (a n)"),
                            pr[:, s1, :, :].rearrange("p a n -> p (a n)"), ALU.add), [exp_tok[g], *acc_free[j]], tok=True)
                        p_free[(g - 1) % NPB].append(d)
                        p_free[sl].append(d)
                        add_tok[0] = d
                    elif t > 1:
                        d = op("vector", lambda e, j=j, s1=sl: e.tensor_tensor(
                            acc[:, j, :], acc[:, j, :], pr[:, s1, :, :].rearrange("p a n -> p (a n)"), ALU.add),
                            [exp_tok[g], add_tok[0]], tok=True)
                        p_free[sl].append(d)
                        add_tok[0] = d
                    if g % 16 == 15:
                        ring_free[r] = [tS]
                        if q + RING < NP:
                            tl_[q + RING] = load_pair(b, q + RING, [])
                    if g % 16 == 8 and q + 1 < NP:
                        t_ring[q + 1] = shift_pair(b, q + 1, t_zero, tl_[q + 1], [exp_tok[g]])
                    if b + 1 < B and g == 100:
                        prefetch_ln(b + 1, 0)
                    tick()
                pv(16 * NP - 1)
                vt_free[:] = [last_pv[0]]
                d1_free = [last_pv[0], add_tok[0]]
            for _ in range(24):
                tick()
            assert not events
            Q.fence([(s_x2, Q.value["s_x2"])])

        with ExitStack() as g2:
            tT = sbuf(g2, "tT", [128, 4, HID], FR)
            tP = sbuf(g2, "tP", [128, 16, E], FR)
            w2s = sbuf(g2, "w2s", [128, HID], FR)
            vth = sbuf(g2, "vth", [128, 4, 128], FR)
            vtl = sbuf(g2, "vtl", [128, 4, 128], FR)
            prow = sbuf(g2, "prow", [128, E])
            scf = sbuf(g2, "scf", [128, 4, 16])
            scp = sbuf(g2, "scp", [128, 4, 4])
            mv2 = sbuf(g2, "mv2", [128, 4, 2])
            st62 = sbuf(g2, "st62", [128, 4, 6])
            rs2 = sbuf(g2, "rs2", [128, 16])
            ln2 = sbuf(g2, "ln2", [128, 24])
            with ExitStack() as al:
                wf = sbuf(al, "wf", [128, 2, HID])
                ta = sbuf(al, "ta", [128, HID])
                tt = sbuf(al, "tt", [128, 2, HID])
                us = sbuf(al, "us", [128, 16, RANK])
                ut = sbuf(al, "ut", [128, 2, 128])
                fba = sbuf(al, "fba", [128, 128])
                fbm = sbuf(al, "fbm", [128, 8, 128])
                vrep = sbuf(al, "vrep", [128, E])
                w2t = sbuf(al, "w2t", [128, 512], FR)
                dg = sbuf(al, "dg", [128, 4, 128])
                on1 = sbuf(al, "on1", [128, 128])
            with ExitStack() as al:
                x2 = sbuf(al, "x2", [128, 2, 4, E])
                xn = sbuf(al, "xn", [128, 4, E])
                yh = sbuf(al, "yh", [128, 2, 4, 512], FR)
                yl = sbuf(al, "yl", [128, 2, 4, 512], FR)
                zt = sbuf(al, "zt", [128, 2, 512], FR)
                zq = sbuf(al, "zq", [128, 512], FR)
                rb = sbuf(al, "rb", [128, 2, 512])
                sb2 = sbuf(al, "sb2", [128, 2, 512])
                hh_ = sbuf(al, "hh_", [128, 3, 512], FR)
                hl_ = sbuf(al, "hl_", [128, 3, 512], FR)
                fo = sbuf(al, "fo", [128, 2, E])

            s_wf = [Q.sem("s_wf0"), Q.sem("s_wf1")]
            s_u = Q.sem("s_u")
            s_fb = Q.sem("s_fb")
            s_x2l = [Q.sem("s_x2l0"), Q.sem("s_x2l1")]
            s_out = [Q.sem("s_out0"), Q.sem("s_out1")]
            bank = {i: [] for i in range(8)}
            wf_free = [[], []]
            tt_free = [[], []]
            tr_n = [0]

            zb = [op("gpsimd", lambda e: e.memset(fba[:], 0.0), tok=True),
                  op("gpsimd", lambda e: e.memset(vrep[:], 0.0), tok=True),
                  op("gpsimd", lambda e: e.memset(on1[:], 1.0), tok=True)]
            wsrc = [w_fc[i * 512:(i + 1) * 512, :].rearrange("(t p) e -> p t e", p=128) for i in range(4)] + \
                   [w_proj[i * 128:(i + 1) * 128, :] for i in range(4)]
            wtok = {}
            for i in range(2):
                dst = wf[:, i, :].rearrange("p (t e) -> p t e", t=4) if i < 4 else wf[:, i % 2, :]
                wtok[i] = dma("sync", s_wf[i], dst, wsrc[i])
            t_u = dma("sync", s_u, us[:], u.rearrange("(t p) r -> p t r", p=128))
            fb4 = fast_b.unsqueeze(1).broadcast_to([RANK, 4, RANK])
            for t8 in range(8):
                t_fb = dma("sync", s_fb, fba[16 * t8:16 * t8 + 16, :].rearrange("p (q c) -> p q c", q=4)[:, :, 0:16], fb4, zb)
            for q4 in range(4):
                t_fb = dma("sync", s_fb, vrep[32 * q4:32 * q4 + 16, :], v, zb)

            ta_free = []
            for i in range(8):
                fc = i < 4
                nt, ln = (4, 512) if fc else (1, 2048)
                bf = i % 2
                for t in range(nt):
                    col = 4 * i + t if fc else i - 4
                    sc = scf if fc else scp
                    wv = wf[:, bf, t * ln:(t + 1) * ln]
                    tv = tt[:, bf, t * ln:(t + 1) * ln]
                    av = ta[:, t * ln:(t + 1) * ln]
                    a = op("scalar", lambda e, av=av, wv=wv, sc=sc, col=col: e.activation(
                        av, wv, ACT.Abs, accum_out=sc[:, 3, col:col + 1]), [wtok[i], *ta_free], tok=True)
                    d = op("vector", lambda e, sc=sc, col=col, ln=ln: e.tensor_scalar(
                        sc[:, 0, col:col + 1], sc[:, 3, col:col + 1], 1.0 / ln, 1e-5, ALU.mult, ALU.max), [a], tok=True)
                    d1 = op("vector", lambda e, sc=sc, col=col: e.tensor_scalar(
                        sc[:, 1, col:col + 1], sc[:, 0, col:col + 1], 0.5, None, ALU.mult), [d], tok=True)
                    d2 = op("vector", lambda e, sc=sc, col=col: e.tensor_scalar(
                        sc[:, 2, col:col + 1], sc[:, 0, col:col + 1], -0.5, None, ALU.mult), [d], tok=True)
                    d3 = op("vector", lambda e, av=av, wv=wv, sc=sc, col=col: e.tensor_scalar(
                        av, wv, sc[:, 2, col:col + 1], None, ALU.is_lt), [d2, a], tok=True)
                    d4 = op("vector", lambda e, av=av, wv=wv, tv=tv, sc=sc, col=col: e.scalar_tensor_tensor(
                        out=tv, in0=wv, scalar=sc[:, 1, col:col + 1], in1=av, op0=ALU.is_gt, op1=ALU.subtract),
                        [d1, d3, *tt_free[bf]], tok=True)
                ta_free = [d4]
                if i + 2 < 8:
                    n2 = i + 2
                    dst = wf[:, bf, :].rearrange("p (t e) -> p t e", t=4) if n2 < 4 else wf[:, bf, :]
                    wtok[n2] = dma("sync", s_wf[bf], dst, wsrc[n2], [d4])
                for m in range(4):
                    bk = tr_n[0] % 8
                    tr_n[0] += 1
                    for k in range(4):
                        tk = op("tensor", lambda e, bk=bk, k=k, m=m, bf=bf: e.transpose(
                            ps[:, bk, k * 128:(k + 1) * 128], tt[:, bf, (4 * m + k) * 128:(4 * m + k + 1) * 128], ident[:]),
                            [d4, t_ident, *bank[bk]], tok=(k == 3))
                    if fc:
                        dst = tT[:, :, (4 * i + m) * 128:(4 * i + m + 1) * 128]
                    else:
                        dst = tP[:, 4 * m:4 * m + 4, (i - 4) * 128:(i - 3) * 128]
                    a = op("scalar", lambda e, dst=dst, bk=bk: e.activation(
                        dst, ps[:, bk, :].rearrange("p (k n) -> p k n", k=4), ACT.Copy), [tk], tok=True)
                    bank[bk] = [a]
                tt_free[bf] = [tk]
            t_tern = a
            for n in range(4):
                d = op("vector", lambda e, n=n: e.tensor_scalar(dg[:, n, :], ident[:], scp[:, 0, n:n + 1], None, ALU.mult),
                       [d4], tok=True)
            tk = op("tensor", lambda e: e.matmul(ps[:, 0, :], on1[:], dg[:].rearrange("p a n -> p (a n)"), start=True,
                    stop=True), [d, *zb, *bank[0]], tok=True)
            t_prow = op("vector", lambda e: e.tensor_copy(prow[:], ps[:, 0, :]), [tk], tok=True)
            bank[0] = [t_prow]
            d = op("vector", lambda e: e.reciprocal(scf[:, 1, :], scf[:, 0, :]), [d4], tok=True)
            d = op("vector", lambda e: e.tensor_scalar(scf[:, 2, :], scf[:, 1, :], gatec, None, ALU.mult), [d, t_gate], tok=True)
            for t in range(16):
                t_us = op("vector", lambda e, t=t: e.tensor_scalar(us[:, t, :], us[:, t, :], scf[:, 2, t:t + 1], None,
                          ALU.mult), [d, t_u], tok=True)
            for t8 in range(8):
                t_fbm = op("vector", lambda e, t8=t8: e.tensor_scalar(fbm[:, t8, :], fba[:], ind[:, t8:t8 + 1], None,
                           ALU.mult), [t_fb, t_ind], tok=True)
            for g in range(2):
                tk = op("tensor", lambda e, g=g: e.transpose(ps[:, 1, g * 128:(g + 1) * 128],
                        us[:, 8 * g:8 * g + 8, :].rearrange("p t r -> p (t r)"), ident[:]), [t_us, *bank[1]], tok=True)
            t_ut = op("vector", lambda e: e.tensor_copy(ut[:].rearrange("p g n -> p (g n)"), ps[:, 1, 0:256]), [tk], tok=True)
            bank[1] = [t_ut]
            w2t_free = []
            for n in range(4):
                bk = 2 + n % 2
                for t in range(4):
                    i = 4 * n + t
                    tk = op("tensor", lambda e, i=i, t=t, bk=bk: e.matmul(ps[:, bk, t * 128:(t + 1) * 128], fbm[:, i % 8, :],
                            ut[:, i // 8, :], start=True, stop=True), [t_ut, t_fbm, *bank[bk]], tok=True)
                cols = slice(n * 512, (n + 1) * 512)
                a = op("scalar", lambda e, bk=bk: e.activation(w2t[:], ps[:, bk, :], ACT.Copy), [tk, *w2t_free], tok=True)
                wl = []
                for q4 in range(4):
                    rw = slice(32 * q4, 32 * q4 + 32)
                    if q4 % 2:
                        wl.append(op("vector", lambda e, rw=rw, cols=cols, bk=bk: e.tensor_tensor(
                            w2s[rw, cols], ps[rw, bk, :], w2t[rw, :], ALU.subtract), [a], tok=True))
                    else:
                        wl.append(op("vector", lambda e, rw=rw, cols=cols, bk=bk: e.tensor_copy(
                            w2s[rw, cols], ps[rw, bk, :]), [a], tok=True))
                bank[bk] = [a, wl[-1]]
                w2t_free = [wl[-1]]
            t_w2s = wl[-1]
            for k in range(4):
                tk = op("tensor", lambda e, k=k: e.transpose(ps[:, 4, k * 128:(k + 1) * 128], vrep[:, k * 128:(k + 1) * 128],
                        ident[:]), [t_fb, *bank[4]], tok=(k == 3))
            vsrc = ps[:, 4, :].rearrange("p (k n) -> p k n", k=4)
            a = op("scalar", lambda e: e.activation(vth[:], vsrc, ACT.Copy), [tk], tok=True)
            t_vt = op("vector", lambda e: e.tensor_tensor(vtl[:], vsrc, vth[:], ALU.subtract), [a], tok=True)
            bank[4] = [a, t_vt]
            Q.fence()

            NB2 = B * S // 512
            bank = {i: [] for i in range(8)}
            x2_free = [[], []]
            xn_free = []
            y_free = [[], []]
            zt_free = [[], []]
            zq_free = []
            rb_free = [[], []]
            sb_free = [[], []]
            hid_free = [[], [], []]
            fo_free = [[], []]
            cnt = {"h": 0, "o": 0}
            x2tok = {}
            lntok = {}
            ytok = {}
            ztok = {}

            def load_rows(n):
                bf = n % 2
                x2tok[n] = dma("sync", s_x2l[bf], x2[:, bf, :, :],
                               x2d[n * 512:(n + 1) * 512, :].rearrange("(t p) e -> p t e", p=128), x2_free[bf])

            def norm_rows(n):
                lntok[n] = layernorm(x2[:, n % 2], xn, mv2, st62, rs2, ln2, 4, [x2tok[n]], xn_free)

            def turn_rows(n, k):
                bf, bk = n % 2, 6 + k % 2
                for st in range(4):
                    tk = op("tensor", lambda e, st=st, k=k, bk=bk: e.transpose(
                        ps[:, bk, st * 128:(st + 1) * 128], xn[:, st, k * 128:(k + 1) * 128], ident[:]),
                        [lntok[n], *bank[bk]], tok=(st == 3))
                a = op("scalar", lambda e: e.activation(yh[:, bf, k, :], ps[:, bk, :], ACT.Copy), [tk, *y_free[bf]], tok=True)
                d = op("vector", lambda e: e.tensor_tensor(yl[:, bf, k, :], ps[:, bk, :], yh[:, bf, k, :], ALU.subtract),
                       [a, *y_free[bf]], tok=True)
                bank[bk] = [a, d]
                xn_free[:] = [tk]
                ytok[n] = d

            def low_rank(n):
                bf = n % 2
                i = 0
                for k in range(4):
                    for w_, y_ in ((vth, yh), (vtl, yh), (vth, yl)):
                        tk = op("tensor", lambda e, k=k, w_=w_, y_=y_, i=i: e.matmul(
                            ps[:, 6, :], w_[:, k, :], y_[:, bf, k, :], start=(i == 0), stop=(i == 11)),
                            [ytok[n], *bank[6]], tok=(i == 11))
                        i += 1
                a1 = op("scalar", lambda e: e.activation(zt[0:64, bf, :], ps[0:64, 6, :], ACT.Copy), [tk, *zt_free[bf]], tok=True)
                a2 = op("scalar", lambda e: e.activation(zq[64:128, :], ps[64:128, 6, :], ACT.Copy), [tk, *zq_free], tok=True)
                d = op("vector", lambda e: e.tensor_tensor(zt[64:128, bf, :], ps[64:128, 6, :], zq[64:128, :], ALU.subtract),
                       [a2, *zt_free[bf]], tok=True)
                zq_free[:] = [d]
                bank[6] = [a1, d]
                ztok[n] = [a1, d]

            def up(n, i):
                bf = n % 2
                h = cnt["h"]
                cnt["h"] += 1
                bk, r2, r3 = 4 + h % 2, h % 2, h % 3
                m = 0
                for k in range(4):
                    for y_ in (yh, yl):
                        op("tensor", lambda e, k=k, y_=y_, m=m: e.matmul(ps[:, bk, :], tT[:, k, i * 128:(i + 1) * 128],
                           y_[:, bf, k, :], start=(m == 0), stop=False), [ytok[n], *bank[bk]])
                        m += 1
                tk = op("tensor", lambda e: e.matmul(ps[:, bk, :], w2s[:, i * 128:(i + 1) * 128], zt[:, bf, :], start=False,
                        stop=True), ztok[n], tok=True)
                a = op("scalar", lambda e: e.activation(rb[:, r2, :], ps[:, bk, :], ACT.Relu, scale=scf[:, 0, i:i + 1]),
                       [tk, *rb_free[r2]], tok=True)
                bank[bk] = [a]
                d = op("vector", lambda e: e.tensor_tensor(sb2[:, r2, :], rb[:, r2, :], rb[:, r2, :], ALU.mult),
                       [a, *sb_free[r2]], tok=True)
                rb_free[r2] = [d]
                a = op("scalar", lambda e: e.activation(hh_[:, r3, :], sb2[:, r2, :], ACT.Copy), [d, *hid_free[r3]], tok=True)
                d = op("vector", lambda e: e.tensor_tensor(hl_[:, r3, :], sb2[:, r2, :], hh_[:, r3, :], ALU.subtract),
                       [a, d, *hid_free[r3]], tok=True)
                sb_free[r2] = [a, d]
                if i == 15:
                    y_free[bf] = [tk]
                    zt_free[bf] = [tk]
                return d, r3

            def down(n, i, hid):
                t_h, r3 = hid
                for rt in range(4):
                    for part, h_ in enumerate((hh_, hl_)):
                        tk = op("tensor", lambda e, rt=rt, h_=h_, part=part: e.matmul(
                            ps[:, rt, :], h_[:, r3, rt * 128:(rt + 1) * 128], tP[:, i, :],
                            start=(i == 0 and part == 0), stop=(i == 15 and part == 1)),
                            [t_h] + (bank[rt] if i == 0 else []), tok=(part == 1 and (rt == 3 or i == 15)))
                    if i == 15:
                        finish(n, rt, tk)
                hid_free[r3] = [tk]

            def finish(n, rt, tk):
                bf = n % 2
                o = cnt["o"] % 2
                cnt["o"] += 1
                d = op("vector", lambda e: e.tensor_tensor(fo[:, o, :], ps[:, rt, :], prow[:], ALU.mult), [tk, *fo_free[o]], tok=True)
                bank[rt] = [d]
                d = op("vector", lambda e: e.tensor_tensor(fo[:, o, :], fo[:, o, :], x2[:, bf, rt, :], ALU.add), [d], tok=True)
                rows = n * 512 + rt * 128
                fo_free[o] = [dma("sync", s_out[o], out_rows[rows:rows + 128, :], fo[:, o, :], [d])]
                if rt == 3:
                    x2_free[bf] = [d]
                    if n + 2 < NB2:
                        load_rows(n + 2)

            out_rows = out.rearrange("b s e -> (b s) e")
            load_rows(0)
            load_rows(1)
            norm_rows(0)
            for k in range(4):
                turn_rows(0, k)
            low_rank(0)
            prev = None
            for n in range(NB2):
                for i in range(16):
                    hid = up(n, i)
                    if prev is not None:
                        down(*prev)
                    prev = (n, i, hid)
                    if n + 1 < NB2:
                        if i == 3:
                            norm_rows(n + 1)
                        if 7 <= i < 11:
                            turn_rows(n + 1, i - 7)
                        if i == 12:
                            low_rank(n + 1)
            down(*prev)
            op("sync", None, [fo_free[0][0], fo_free[1][0]])

        with nc.Block() as block:
            Q.play(block)


_INS = ['L0_attn_x', 'L0_attn_w_qkv', 'L0_attn_wo', 'L0_attn_lambda_q1', 'L0_attn_lambda_q2', 'L0_attn_lambda_k1',
        'L0_attn_lambda_k2', 'L0_attn_norm_w', 'L0_ffn_fast_b', 'L0_ffn_w_fc', 'L0_ffn_w_proj', 'L0_ffn_u', 'L0_ffn_v',
        'L0_ffn_gate']
_OUTS = [((B, S, E), 'float32')]


def kernel(**inputs):
    import numpy as _np
    import concourse.bacc as _bacc
    from concourse import mybir as _mybir
    from concourse.bass_utils import run_bass_kernel_spmd as _run

    nc = _bacc.Bacc("TRN2", target_bir_lowering=False, num_devices=1)
    arrays, args = {}, []
    for name in _INS:
        a = _np.ascontiguousarray(inputs[name])
        arrays[f"in_{name}_dram"] = a
        args.append(nc.dram_tensor(f"in_{name}_dram", a.shape, _mybir.dt.from_np(a.dtype), kind="ExternalInput").ap())
    for i, (shape, dtype) in enumerate(_OUTS):
        dt = _mybir.dt.from_np(_np.dtype(dtype))
        args.append(nc.dram_tensor(f"out_{i}_dram", shape, dt, kind="ExternalOutput").ap())
    build(nc, *args)
    r = _run(nc, [arrays], core_ids=[0])
    got = tuple(r.results[0][f"out_{i}_dram"] for i in range(len(_OUTS)))
    return got[0]
```

```python
import numpy as np
import concourse.bass as bass
from concourse import mybir
from contextlib import ExitStack

F32 = mybir.dt.float32
FR = mybir.dt.float32r
BF16 = mybir.dt.bfloat16
I32 = mybir.dt.int32
ALU = mybir.AluOpType
ACT = mybir.ActivationFunctionType
AX = mybir.AxisListType

B, S, E, H, HD = 8, 1024, 512, 16, 32
HID, RANK = 2048, 16
NP = H // 2
SCALE = float(1.0 / np.sqrt(np.float32(HD)))
LAMBDA_INIT = 0.8
RING = 2
NPB = 4
LAG = 2
SAFE = 32.0


class Queues:

    ENGINES = ("tensor", "scalar", "vector", "gpsimd", "sync")

    def __init__(self, nc, ctx):
        self.nc, self.ctx = nc, ctx
        self.items = {e: [] for e in self.ENGINES}
        self.value = {}
        self.done = {e: self.sem("s_" + e) for e in self.ENGINES[:4]}

    def sem(self, name):
        s = self.ctx.enter_context(self.nc.semaphore(name))
        self.value[name] = 0
        return (name, s)

    def op(self, engine, fn, waits=(), tok=False):
        sem = self.done[engine] if tok else None
        self.items[engine].append((fn, [w for w in waits if w is not None], sem, 1))
        if tok:
            self.value[sem[0]] += 1
            return (sem, self.value[sem[0]])
        return None

    def dma(self, engine, sem, dst, src, waits=(), **how):
        self.items[engine].append((lambda e: e.dma_start(dst, src, **how), [w for w in waits if w is not None], sem, 16))
        self.value[sem[0]] += 16
        return (sem, self.value[sem[0]])

    def expect(self, sem, n):
        self.value[sem[0]] += n
        return (sem, self.value[sem[0]])

    def fence(self, extra=()):
        toks = [self.op(e, lambda eng: eng.drain(), tok=True) for e in self.ENGINES[:4]]
        for e in self.ENGINES:
            self.op(e, None, toks + list(extra))

    def play(self, block):
        at = {"tensor": block.tensor, "scalar": block.scalar, "vector": block.vector, "gpsimd": block.gpsimd,
              "sync": block.sync}

        def body(name):
            def run(eng):
                seen = {}
                for fn, waits, sem, inc in self.items[name]:
                    for (wname, wsem), v in waits:
                        if seen.get(wname, 0) < v:
                            eng.wait_ge(wsem, v)
                            seen[wname] = v
                    if fn is None:
                        continue
                    ins = fn(eng)
                    if sem is not None:
                        ins.then_inc(sem[1], inc)
            at[name](run)
        for name in self.ENGINES:
            body(name)


def build(nc, x, wqkv, wo, lq1, lq2, lk1, lk2, norm_w, fast_b, w_fc, w_proj, u, v, gate, out):
    x2d = nc.dram_tensor("x2_scratch", [B * S, E], F32, kind="Internal").ap()
    qsc = nc.dram_tensor("q_scratch", [2, 4, 8, 3, 16, S], BF16, kind="Internal").ap()
    ksc = nc.dram_tensor("k_scratch", [2, 4, 8, 3, 16, S], BF16, kind="Internal").ap()

    with ExitStack() as top:
        Q = Queues(nc, top)
        op, dma = Q.op, Q.dma
        ps = top.enter_context(nc.psum_tensor("ps", [128, 8, 512], F32))

        def sbuf(ctx, name, shape, dt=F32):
            return ctx.enter_context(nc.sbuf_tensor(name, shape, dt))

        ident = sbuf(top, "ident", [128, 128])
        small = sbuf(top, "small", [128, 64])
        ind = sbuf(top, "ind", [128, 8])
        scf = sbuf(top, "scf", [128, 4, 16])
        scp = sbuf(top, "scp", [128, 4, 4])
        eps5, eps6, neglam, gatec = small[:, 0:1], small[:, 1:2], small[:, 2:3], small[:, 3:4]

        op("scalar", lambda e: (e.preload_act_table_set("natural_log_exp_and_others"), None)[1])
        t_c0 = [op("gpsimd", lambda e: e.memset(ident[:], 0.0), tok=True),
                op("gpsimd", lambda e: e.memset(ind[:], 1.0), tok=True)]
        t_ident = op("gpsimd", lambda e: e.affine_select(out=ident[:], in_=ident[:], compare_op=ALU.not_equal, fill=1.0,
                     base=0, pattern=[[-1, 128]], channel_multiplier=1), [t_c0[0]], tok=True)
        t_i1 = op("gpsimd", lambda e: e.affine_select(out=ind[:], in_=ind[:], compare_op=ALU.is_ge, fill=0.0,
                  base=0, pattern=[[-16, 8]], channel_multiplier=1), [t_c0[1]], tok=True)
        t_ind = op("gpsimd", lambda e: e.affine_select(out=ind[:], in_=ind[:], compare_op=ALU.is_ge, fill=0.0,
                   base=15, pattern=[[16, 8]], channel_multiplier=-1), [t_i1], tok=True)
        t_eps = [op("gpsimd", lambda e: e.memset(eps5, 1e-5), tok=True),
                 op("gpsimd", lambda e: e.memset(eps6, 1e-6), tok=True)]
        s_small = Q.sem("s_small")
        t_gate = dma("sync", s_small, gatec, gate.partition_broadcast(128))

        ln_prev = []

        def layernorm(xin, xout, mv, st6, rs, ln_t, n, waits, put, wout=()):
            t = []
            var = mv[:, 0:n, 1]
            h = ln_t[:, 8:8 + n]
            g = ln_t[:, 16:16 + n]

            def stats(i):
                t.append(op("vector", lambda e: e.bn_stats(st6[:, i, :], xin[:, i, :]), [*waits, *ln_prev], tok=True))

            def gather():
                for i in range(n):
                    a = op("vector", lambda e, i=i: e.bn_aggr(mv[:, i, :], st6[:, i, :]), [t[i]], tok=True)
                t[:] = [a]

            def scale():
                a = t[0]
                l1 = op("scalar", lambda e: e.activation(ln_t[:, 0:n], var, ACT.Ln, bias=eps5), [a] + t_eps, tok=True)
                l2 = op("scalar", lambda e: e.activation(rs[:, 0:n], ln_t[:, 0:n], ACT.Exp, scale=-0.5), [l1], tok=True)
                t[:] = [a, l2]

            def newton():
                a, l2 = t
                c1 = op("vector", lambda e: e.tensor_tensor(h, rs[:, 0:n], rs[:, 0:n], ALU.mult), [l2], tok=True)
                c2 = op("vector", lambda e: e.tensor_scalar(g, var, 1e-5, -0.5, ALU.add, ALU.mult), [a], tok=True)
                c3 = op("vector", lambda e: e.tensor_tensor(h, h, g, ALU.mult), [c1, c2], tok=True)
                c4 = op("vector", lambda e: e.scalar_tensor_tensor(out=rs[:, 8:8 + n], in0=h, scalar=1.5, in1=rs[:, 0:n],
                        op0=ALU.add, op1=ALU.mult), [c3], tok=True)
                t[:] = [c4]

            def apply(i):
                last = op("vector", lambda e: e.tensor_scalar(xout[:, i, :], xin[:, i, :], mv[:, i, 0:1],
                          rs[:, 8 + i:9 + i], ALU.subtract, ALU.mult), [t[0], *wout], tok=True)
                if i == n - 1:
                    ln_prev[:] = [last]
                    put(last)

            return [lambda i=i: stats(i) for i in range(n)] + [gather, scale, newton] + [lambda i=i: apply(i) for i in range(n)]

        with ExitStack() as g1:
            with ExitStack() as al:
                wf = sbuf(al, "wf", [128, 3, HID])
                ta = sbuf(al, "ta", [128, 2, HID])
            wqh = sbuf(g1, "wqh", [128, 4, 3 * E], FR)
            wql = sbuf(g1, "wql", [128, 4, 3 * E], FR)
            woh = sbuf(g1, "woh", [128, 4, E], FR)
            wol = sbuf(g1, "wol", [128, 4, E], FR)
            qst = sbuf(g1, "qst", [128, RING, 4, S], BF16)
            kst = sbuf(g1, "kst", [128, RING, 4, S], BF16)
            vt = sbuf(g1, "vt", [128, 8, E])
            acc = sbuf(g1, "acc", [128, 2, 2 * S])
            xin = sbuf(g1, "xin", [128, 4, E])
            xth = sbuf(g1, "xth", [128, 4, 512], FR)
            xtl = sbuf(g1, "xtl", [128, 4, 512], FR)
            rl = sbuf(g1, "rl", [128, 2, E])
            ot = sbuf(g1, "ot", [128, E])
            sq = sbuf(g1, "sq", [128, E])
            oth = sbuf(g1, "oth", [128, 4, 128], FR)
            otl = sbuf(g1, "otl", [128, 4, 128], FR)
            xr = sbuf(g1, "xr", [128, E])
            sqb = sbuf(g1, "sqb", [128, 3, E], BF16)
            indb = sbuf(g1, "indb", [128, 8], BF16)
            blk = sbuf(g1, "blk", [128, 128])
            ones = sbuf(g1, "ones", [128, 32])
            nw = sbuf(g1, "nw", [128, NP])
            mx = sbuf(g1, "mx", [128, 128])
            mh = sbuf(g1, "mh", [32, 3, 128], BF16)
            mr = sbuf(g1, "mr", [32, 128])
            mv = sbuf(g1, "mv", [128, 4, 2])
            st6 = sbuf(g1, "st6", [128, 4, 6])
            rs = sbuf(g1, "rs", [128, 16])
            ln_t = sbuf(g1, "ln_t", [128, 24])
            nmx = sbuf(g1, "nmx", [8, 40])
            fl = sbuf(g1, "fl", [1, 1], I32)
            lam = sbuf(g1, "lam", [128, 4, HD])
            with ExitStack() as al:
                pr = sbuf(al, "pr", [128, NPB, 2, S])
            with ExitStack() as al:
                hml = sbuf(al, "hml", [128, 4, 3, 512], BF16)
                r1 = sbuf(al, "r1", [128, 2, 512])
            with ExitStack() as al:
                wst = sbuf(al, "wst", [128, 4, 3 * E])

            s_wf = [Q.sem(f"s_wf{k}") for k in range(3)]
            wsrc = [w_fc[i * 512:(i + 1) * 512, :].rearrange("(t p) e -> p t e", p=128) for i in range(4)] + \
                   [w_proj[i * 128:(i + 1) * 128, :] for i in range(4)]
            wtok, abs_tok, ta_free = {}, {}, [[], []]

            def parts(i):
                if i < 4:
                    return [(scf, 4 * i + t, slice(t * 512, t * 512 + 512)) for t in range(4)]
                return [(scp, i - 4, slice(0, 2048))]

            def load_weights(i, waits):
                dst = wf[:, i % 3, :].rearrange("p (t e) -> p t e", t=4) if i < 4 else wf[:, i % 3, :]
                wtok[i] = dma("sync", s_wf[i % 3], dst, wsrc[i], waits)

            def magnitudes(i, waits):
                for sc, col, c in parts(i):
                    abs_tok[i] = op("scalar", lambda e, sc=sc, col=col, c=c: e.activation(
                        ta[:, i % 2, c], wf[:, i % 3, c], ACT.Abs, accum_out=sc[:, 3, col:col + 1]),
                        [wtok[i], *ta_free[i % 2], *waits], tok=True)

            s_w = [Q.sem(f"s_w{k}") for k in range(4)]
            s_wo = Q.sem("s_wo")
            s_x = Q.sem("s_x")
            s_hml = [Q.sem(f"s_hml{i}") for i in range(4)]
            s_ring = [Q.sem(f"s_ring{i}") for i in range(RING)]
            s_mh = Q.sem("s_mh")
            s_xr = Q.sem("s_xr")
            s_x2 = Q.sem("s_x2")
            s_gpe = Q.sem("s_gpe")
            s_gdve = Q.sem("s_gdve")

            def x_chunk(b, c):
                return x[b, c * 512:(c + 1) * 512, :].rearrange("(t p) e -> p t e", p=128)

            t_x = dma("sync", s_x, xin[:], x_chunk(0, 0))
            wqk = wqkv.rearrange("(k p) n -> p k n", p=128)
            t_w = [dma("sync", s_w[k], wst[:, k, :], wqk[:, k, :]) for k in range(4)]
            for i, l in enumerate((lq1, lk1, lq2, lk2)):
                t_lam = dma("sync", s_small, lam[:, i, :], l.partition_broadcast(128))
            nwr = norm_w.rearrange("(p h) d -> h d p", h=2)
            for i in range(4):
                t_nw = dma("sync", s_small, nw[32 * i:32 * i + 32, :], nwr[i // 2], allow_slow_non_contiguous=True)
            for k in range(4):
                t_wh = op("scalar", lambda e, k=k: e.activation(wqh[:, k, :], wst[:, k, :], ACT.Copy), [t_w[k]], tok=True)
                t_wl = op("vector", lambda e, k=k: e.tensor_tensor(wql[:, k, :], wst[:, k, :], wqh[:, k, :], ALU.subtract),
                          [t_wh], tok=True)
            wos = acc[:, 0, :].rearrange("p (k n) -> p k n", k=4)
            t_w2 = dma("sync", s_wo, wos, wo.rearrange("(k p) n -> p k n", p=128))
            dt_ = small[:, 8:16]
            tl = [op("vector", lambda e, i=i: e.tensor_tensor(lam[:, 2 * i, :], lam[:, 2 * i, :], lam[:, 2 * i + 1, :],
                     ALU.mult), [t_nw], tok=True) for i in range(2)]
            tl = [op("vector", lambda e, i=i: e.tensor_reduce(dt_[:, i:i + 1], lam[:, 2 * i, :], AX.X, ALU.add),
                     [tl[i]], tok=True) for i in range(2)]
            t_le = op("scalar", lambda e: e.activation(dt_[:, 2:4], dt_[:, 0:2], ACT.Exp), tl, tok=True)
            t_ld = op("vector", lambda e: e.tensor_tensor(dt_[:, 4:5], dt_[:, 3:4], dt_[:, 2:3], ALU.subtract), [t_le], tok=True)
            t_lam = op("vector", lambda e: e.tensor_scalar(neglam, dt_[:, 4:5], -LAMBDA_INIT, None, ALU.add), [t_ld], tok=True)
            t_nw = op("vector", lambda e: e.tensor_scalar(nw[:], nw[:], 1.0 - LAMBDA_INIT, None, ALU.mult), [t_nw], tok=True)
            t_indb = op("vector", lambda e: e.tensor_copy(indb[:], ind[:]), [t_ind], tok=True)
            tc = [op("vector", lambda e: e.memset(blk[:], 0.0), tok=True),
                  op("vector", lambda e: e.memset(ones[:], 1.0), tok=True),
                  op("vector", lambda e: e.memset(mx[:], 0.0), tok=True),
                  op("vector", lambda e: e.memset(kst[96:128, :, :, :], 1.0), tok=True)]
            for i in range(4):
                t_blk = op("vector", lambda e, i=i: e.memset(blk[32 * i:32 * i + 32, 32 * i:32 * i + 32], 1.0), [tc[0]], tok=True)
            t_ones = tc[3]

            bank = {i: [] for i in range(8)}
            p_free = [[t_wl, t_wh] for _ in range(NPB)]
            d1_free = [t_wl, t_wh]
            acc_free = [[], []]
            ring_free = [[] for _ in range(RING)]
            hml_free = [[] for _ in range(4)]
            vt_free = []
            mh_free = []
            r_free = [[], []]
            xr_free = []
            sq_free = []
            ot_free = []
            ot_w = []
            r1_free = [[], []]
            ott_free = []
            sqb_free = [[], [], []]
            xin_free = []
            xt_free = []
            xt_tok = {}
            events = {}
            slot = [0]
            dense = [True]

            def at(delay, fn):
                events.setdefault(slot[0] + delay, []).append(fn)

            def tick():
                if dense[0]:
                    filler()
                for fn in events.pop(slot[0], []):
                    fn()
                slot[0] += 1

            fill = []
            urgent = []
            pairs_in, turned, normed = [0], [0], [0]

            busy = {6: False, 7: False}
            queue = {6: [], 7: []}

            def with_bank(bk, fn):
                if busy[bk]:
                    queue[bk].append(fn)
                else:
                    busy[bk] = True
                    fn(bk)

            def read(bk, toks):
                bank[bk] = toks
                busy[bk] = False
                if queue.get(bk):
                    busy[bk] = True
                    at(1, lambda fn=queue[bk].pop(0): fn(bk))

            def filler():
                if urgent:
                    urgent.pop(0)()
                elif fill:
                    fill.pop(0)()

            reg = {}

            def turn(k, bk, t_ln, early):
                for st in range(4):
                    t = op("tensor", lambda e, st=st: e.transpose(
                        ps[:, bk, st * 128:(st + 1) * 128], xin[:, st, k * 128:(k + 1) * 128], ident[:]),
                        [t_ln, t_ident, *bank[bk]], tok=(st == 3))

                def out():
                    a = op("scalar", lambda e: e.activation(xth[:, k, :], ps[:, bk, :], ACT.Copy), [t, *xt_free], tok=True)
                    d = op("vector", lambda e: e.tensor_tensor(xtl[:, k, :], ps[:, bk, :], xth[:, k, :], ALU.subtract),
                           [a, *xt_free], tok=True)
                    xt_tok[k] = d
                    xin_free[:] = [t]
                    read(bk, [a, d])
                if early:
                    at(1, out)
                else:
                    out()

            def project(dst, mcol, lhs, waits):
                n = 0
                for k in range(4):
                    for w, xx in ((wqh, xth), (wql, xth), (wqh, xtl)):
                        if lhs == "w":
                            f = lambda e, k=k, w=w, xx=xx, n=n: e.matmul(
                                dst, w[:, k, mcol:mcol + 128], xx[:, k, :], start=(n == 0), stop=(n == 11))
                        else:
                            f = lambda e, k=k, w=w, xx=xx, n=n: e.matmul(
                                dst, xx[:, k, lhs * 128:(lhs + 1) * 128], w[:, k, mcol:mcol + 512],
                                start=(n == 0), stop=(n == 11))
                        t = op("tensor", f, [*waits, xt_tok[k]], tok=(n == 11))
                        n += 1
                return t

            mcount = [0]
            vcount = [0]

            def qk_tile(b, c, m):
                i = mcount[0]
                mcount[0] += 1
                bk = i % 4
                t = project(ps[:, bk, :], m * 128, "w", [t_wl, *bank[bk]])
                hb, rb_, qb = i % 4, i % 2, i % 3
                p = ps[:, bk, :]
                h_, m_, l_ = (hml[:, hb, j, :] for j in range(3))
                a = op("scalar", lambda e: e.activation(h_, p, ACT.Copy), [t, *hml_free[hb], *d1_free], tok=True)
                d1 = op("vector", lambda e: e.tensor_tensor(r1[:, rb_, :], p, h_, ALU.subtract), [a, *d1_free, *r1_free[rb_]], tok=True)
                d2 = op("vector", lambda e: e.tensor_copy(m_, r1[:, rb_, :]), [d1], tok=True)
                d3 = op("vector", lambda e: e.tensor_tensor(l_, r1[:, rb_, :], m_, ALU.subtract), [d2], tok=True)
                g = op("scalar", lambda e: e.activation(sqb[:, qb, :], h_, ACT.Square), [a, *sqb_free[qb]], tok=True)
                bank[bk] = [a, d1]
                r1_free[rb_] = [d3]
                sc = (qsc if m < 4 else ksc)[b % 2, m % 4]
                order = (0, 1, 2) if m < 4 else (2, 1, 0)
                for cc, part in enumerate(order):
                    td = dma("sync", s_hml[hb], sc[:, cc, :, c * 512:(c + 1) * 512], hml[:, hb, part, :], [a, d3])
                hml_free[hb] = [td, g]
                nb = 4

                def norms():
                    tn = op("tensor", lambda e: e.matmul(ps[0:8, nb, :], indb[:], sqb[:, qb, :], start=True, stop=True),
                            [g, t_indb, *bank[nb]], tok=True)
                    dn = op("vector", lambda e: e.tensor_reduce(nmx[0:8, c * 8 + m:c * 8 + m + 1], ps[0:8, nb, :], AX.X,
                            ALU.max), [tn], tok=True)
                    bank[nb] = [dn]
                    sqb_free[qb] = [tn]
                    return dn
                return norms, td

            def v_tile(c, st):
                i = mcount[0]
                mcount[0] += 1
                bk = i % 4
                t = project(ps[:, bk, :], 2 * E, st, [t_wl, *bank[bk]])
                a = op("scalar", lambda e: e.activation(vt[:, c * 4 + st, :], ps[:, bk, :], ACT.Copy),
                       [t, *vt_free], tok=True)
                bank[bk] = [a]
                return t, a

            def flag(t_n):
                a = op("vector", lambda e: e.tensor_tensor(nmx[:, 16:24], nmx[:, 0:8], nmx[:, 8:16], ALU.max), [t_n], tok=True)
                a = op("vector", lambda e: e.tensor_tensor(nmx[:, 24:28], nmx[:, 16:20], nmx[:, 20:24], ALU.mult), [a], tok=True)
                a = op("vector", lambda e: e.tensor_scalar(nmx[:, 28:32], nmx[:, 24:28], (SAFE / SCALE) ** 2, None,
                       ALU.is_gt), [a], tok=True)
                a = op("vector", lambda e: e.tensor_reduce(nmx[:, 32:33], nmx[:, 28:32], AX.X, ALU.max), [a], tok=True)
                t = op("tensor", lambda e: e.matmul(ps[0:1, 4, 0:1], nmx[0:8, 32:33], ones[0:8, 0:1], start=True, stop=True),
                       [a, t_ones, *bank[4]], tok=True)
                d = op("vector", lambda e: e.tensor_copy(fl[:], ps[0:1, 4, 0:1]), [t], tok=True)
                bank[4] = [d]
                z = op("vector", lambda e: e.memset(mh[:], 0.0), mh_free, tok=True)
                mh_free.clear()

                def load(name):
                    def fn(e):
                        reg[name] = e.value_load(fl[0:1, 0:1], min_val=0, max_val=8)
                    return fn
                op("tensor", load("tensor"), [d])
                op("vector", load("vector"), [d])
                return z

            def load_pair(b, q, t_sc):
                r = (b * NP + q) % RING
                tile, s0 = q // 2, 4 * (q % 2)
                w = [*t_sc, *ring_free[r]]
                row = 0
                for n in (3, 2, 1):
                    for dst, sc, c0 in ((qst, qsc, 0), (kst, ksc, 3 - n)):
                        t = dma("sync", s_ring[r], dst[row:row + 16 * n, r, :, :],
                                sc[b % 2, tile, s0:s0 + 4, c0:c0 + n].rearrange("s c d n -> (c d) s n"), w)
                    row += 16 * n
                return t

            def shift_pair(b, q, t_zero, t_stack, t_act):
                r = (b * NP + q) % RING
                base_pe, base_dve = Q.value["s_gpe"], Q.value["s_gdve"]
                spe, sdve = s_gpe[1], s_gdve[1]
                n_pe, n_dve = 33, 36
                prev_mh = list(mh_free)
                before = [*t_act, t_stack] + [w for bk in range(4) for w in bank[bk]]

                def pe(e):
                    with e.If(reg["tensor"] > 0):
                        for (_, ws), v_ in before:
                            e.wait_ge(ws, v_)
                        for i in range(32):
                            sl, st = i // 8, i % 8
                            if i >= 2:
                                e.wait_ge(sdve, base_dve + i - 1)
                            for c in range(2):
                                l = e.matmul(ps[:, 2 * (i % 2) + c, :], qst[0:96, r, sl, st * 128:(st + 1) * 128],
                                             kst[0:96, r, sl, c * 512:(c + 1) * 512], start=True, stop=True)
                            l.then_inc(spe, 1)
                        e.wait_ge(sdve, base_dve + 32)
                        e.transpose(ps[:, 0, 0:128], mx[:], ident[:]).then_inc(spe, 1)
                        e.wait_ge(sdve, base_dve + n_dve)
                    with e.Else():
                        e.sem_inc(spe, n_pe)

                def dve(e):
                    with e.If(reg["vector"] > 0):
                        for (_, ws), v_ in prev_mh:
                            e.wait_ge(ws, v_)
                        for i in range(32):
                            e.wait_ge(spe, base_pe + i + 1)
                            e.tensor_reduce(mx[:, i:i + 1], ps[:, 2 * (i % 2):2 * (i % 2) + 2, :], AX.XY, ALU.max)\
                                .then_inc(sdve, 1)
                        e.wait_ge(spe, base_pe + 33)
                        e.tensor_scalar(mh[:, 0, :], ps[0:32, 0, 0:128], -1.0, None, ALU.mult).then_inc(sdve, 1)
                        e.wait_ge(sdve, base_dve + 33)
                        e.scalar_tensor_tensor(out=mr[:], in0=ps[0:32, 0, 0:128], scalar=-1.0, in1=mh[:, 0, :],
                                               op0=ALU.mult, op1=ALU.subtract).then_inc(sdve, 1)
                        e.wait_ge(sdve, base_dve + 34)
                        e.tensor_copy(mh[:, 1, :], mr[:]).then_inc(sdve, 1)
                        e.wait_ge(sdve, base_dve + 35)
                        e.tensor_tensor(mh[:, 2, :], mr[:], mh[:, 1, :], ALU.subtract).then_inc(sdve, 1)
                    with e.Else():
                        e.sem_inc(sdve, n_dve)

                op("tensor", pe)
                op("vector", dve)
                Q.expect(s_gpe, n_pe)
                t_m = Q.expect(s_gdve, n_dve)
                for c in range(3):
                    t = dma("sync", s_ring[r], qst[96 + c:97 + c, r, :, :].rearrange("o s (t i) -> o (s t) i", i=128),
                            mh[:, c, :], [t_m, t_zero, *ring_free[r]])
                mh_free[:] = [t]
                return t

            def post_half(b, p, j, t_pv, t_acc):
                st = {}

                def p_l(a0):
                    st["bl"] = a0

                    def piece(n):
                        for c4 in range(4):
                            a = c4 * 512 + n * 256
                            t = op("tensor", lambda e, c4=c4, a=a: e.matmul(
                                ps[32 * c4:32 * c4 + 32, a0, n * 256:n * 256 + 256], ones[:], acc[:, j, a:a + 256],
                                start=(n == 0), stop=True, skip_group_check=True),
                                [t_acc, t_ones] + (bank[a0] if n == 0 else []), tok=(c4 == 3))
                        if n == 1:
                            st["l"] = t
                            acc_free[j] = [t]
                            at(1, p_r)
                    urgent.append(lambda: piece(0))
                    urgent.append(lambda: piece(1))

                def p_r():
                    a0 = st["bl"]
                    a = op("scalar", lambda e: e.activation(rl[:, j, :], ps[:, a0, :], ACT.Ln), [st["l"], *r_free[j]], tok=True)
                    read(a0, [a])
                    a = op("scalar", lambda e: e.activation(rl[:, j, :], rl[:, j, :], ACT.Exp, scale=-1.0), [a], tok=True)
                    st["r"] = a
                    at(1, p_t)

                def p_t():
                    if j == 0:
                        t = op("vector", lambda e: e.tensor_tensor(rl[:, 0, :], ps[:, 4, :], rl[:, 0, :], ALU.mult),
                               [t_pv, st["r"]], tok=True)
                        bank[4] = [t]
                        ot_w[:] = [t]
                        return
                    assert normed[0] == b * NP + p
                    t = op("vector", lambda e: e.scalar_tensor_tensor(out=ot[:], in0=ps[:, 5, :], scalar=neglam,
                           in1=rl[:, 1, :], op0=ALU.mult, op1=ALU.mult), [t_pv, st["r"], t_lam, *ot_free], tok=True)
                    bank[5] = [t]
                    r_free[1] = [t]
                    t = op("vector", lambda e: e.tensor_tensor(ot[:], ot[:], rl[:, 0, :], ALU.add), [t, *ot_w], tok=True)
                    r_free[0] = [t]
                    st["o"] = t
                    at(3, p_sq)

                def p_sq():
                    assert turned[0] == b * NP + p
                    st["s"] = op("scalar", lambda e: e.activation(sq[:], ot[:], ACT.Square), [st["o"], *sq_free], tok=True)
                    at(1, lambda: with_bank(7, p_rms))

                def p_rms(a0):
                    st["bm"] = a0

                    def piece(n):
                        c = slice(n * 256, n * 256 + 256)
                        t = op("tensor", lambda e: e.matmul(ps[:, a0, c], blk[:], sq[:, c], start=(n == 0), stop=True,
                               skip_group_check=True), [st["s"], t_blk] + (bank[a0] if n == 0 else []), tok=True)
                        if n == 1:
                            st["m"] = t
                            at(3, p_rr)
                    urgent.append(lambda: piece(0))
                    urgent.append(lambda: piece(1))

                def p_rr():
                    a0 = st["bm"]
                    a = op("scalar", lambda e: e.activation(sq[:], ps[:, a0, :], ACT.Ln, bias=eps6, scale=1.0 / HD),
                           [st["m"], *t_eps], tok=True)
                    read(a0, [a])
                    a = op("scalar", lambda e: e.activation(sq[:], sq[:], ACT.Exp, scale=-0.5), [a], tok=True)
                    st["rr"] = a
                    at(1, p_on)

                def p_on():
                    t = op("vector", lambda e: e.scalar_tensor_tensor(out=sq[:], in0=ot[:], scalar=nw[:, p:p + 1], in1=sq[:],
                           op0=ALU.mult, op1=ALU.mult), [st["rr"], st["o"], t_nw], tok=True)
                    ot_free[:] = [t, st["s"]]
                    normed[0] += 1
                    st["on"] = t
                    at(1, lambda: with_bank(6, lambda bk: urgent.append(lambda: p_tr(bk))))

                def p_tr(a0):
                    st["bt"] = a0
                    for k in range(4):
                        t = op("tensor", lambda e, k=k: e.transpose(ps[:, a0, k * 128:(k + 1) * 128],
                               sq[:, k * 128:(k + 1) * 128], ident[:]), [st["on"], *bank[a0]], tok=(k == 3))
                    sq_free[:] = [t]
                    turned[0] += 1
                    st["tr"] = t
                    at(1, p_hl)

                def p_hl():
                    a0 = st["bt"]
                    src = ps[:, a0, :].rearrange("p (k n) -> p k n", k=4)
                    a = op("scalar", lambda e: e.activation(oth[:], src, ACT.Copy), [st["tr"], *ott_free], tok=True)
                    d = op("vector", lambda e: e.tensor_tensor(otl[:], src, oth[:], ALU.subtract), [a, *ott_free], tok=True)
                    read(a0, [a, d])
                    st["hl"] = d
                    assert pairs_in[0] == b * NP + p
                    at(2, lambda: with_bank(6, p_wo))

                def p_wo(a0):
                    st["bw"] = a0
                    st["xr"] = dma("sync", s_xr, xr[:], x[b].rearrange("(d g) e -> g d e", g=32)[4 * p:4 * p + 4], xr_free)
                    todo = [(k, o_, w_) for k in range(4) for o_, w_ in ((oth, woh), (oth, wol), (otl, woh))]

                    def piece(m):
                        for n in range(m, m + 3):
                            k, o_, w_ = todo[n]
                            t = op("tensor", lambda e, k=k, o_=o_, w_=w_, n=n: e.matmul(
                                ps[:, a0, :], o_[:, k, :], w_[:, k, :], start=(n == 0), stop=(n == 11)),
                                [st["hl"], t_wol] + (bank[a0] if n == 0 else []), tok=(n == 11))
                        if m + 3 == 12:
                            ott_free[:] = [t]
                            pairs_in[0] += 1
                            st["wo"] = t
                            at(1, p_x2)
                    for m in range(0, 12, 3):
                        fill.append(lambda m=m: piece(m))

                def p_x2():
                    rows = x2d[b * S:(b + 1) * S, :].rearrange("(d g) e -> g d e", g=32)[4 * p:4 * p + 4]
                    a0 = st["bw"]
                    d = op("vector", lambda e: e.tensor_tensor(xr[:], ps[:, a0, :], xr[:], ALU.add),
                           [st["wo"], st["xr"]], tok=True)
                    read(a0, [d])
                    t = dma("sync", s_x2, rows, xr[:], [d])
                    xr_free[:] = [t]

                at(1, lambda: with_bank(7, p_l))

            ln_tok = {}

            def prefetch_x(b, c):
                ln_tok["x"] = dma("sync", s_x, xin[:], x_chunk(b, c), xin_free)

            def prefetch_ln(b, c):
                return layernorm(xin, xin, mv, st6, rs, ln_t, 4, [ln_tok["x"]], lambda t: ln_tok.update(ln=t))

            ln_tok["x"] = t_x
            for step in prefetch_ln(0, 0):
                step()
            for b in range(B):
                t_sc = {}
                pend = []
                t_n = None
                for c in range(2):
                    if c == 1 or b == 0:
                        for k in range(4):
                            turn(k, k, ln_tok["ln"], False)
                    if c == 0:
                        prefetch_x(b, 1)
                        if b == 0:
                            t_woh = op("scalar", lambda e: e.activation(woh[:], wos, ACT.Copy), [t_w2], tok=True)
                            t_wol = op("vector", lambda e: e.tensor_tensor(wol[:], wos, woh[:], ALU.subtract),
                                       [t_woh], tok=True)
                            acc_free[0] = [t_wol]
                    for m in (0, 4, 1, 5, 2, 6, 3, 7):
                        nrm, td = qk_tile(b, c, m)
                        t_sc.setdefault(m % 4, []).append(td)
                        if c == 1 and m == 5:
                            tl_ = {q: load_pair(b, q, t_sc[0]) for q in range(RING)}
                        pend.append(nrm)
                        if len(pend) > 2:
                            pend.pop(0)()
                        tick()
                    if c == 0:
                        steps = prefetch_ln(b, 1)
                    for st in range(4):
                        t_vp, t_va = v_tile(c, st)
                        if pend:
                            t_n = pend.pop(0)()
                        if c == 0:
                            for step in steps[:3]:
                                step()
                            steps = steps[3:]
                        if c == 1 and st == 2:
                            t_zero = flag(t_n)
                        tick()
                    xt_free[:] = [t_vp]
                d1_end = [t_vp] + [w for f in hml_free for w in f]
                for s in range(NPB):
                    p_free[s] = list(d1_end)
                dense[0] = False
                exp_tok = {}
                s_tok = [None, None]
                last_pv = [None]
                t_ring = {0: shift_pair(b, 0, t_zero, tl_[0], [])}
                if b + 1 < B:
                    prefetch_x(b + 1, 0)
                else:
                    for i in range(3):
                        load_weights(i, [t_vp])
                add_tok = [None]
                sum_tok = {}

                def pv(g, half):
                    q, j, t = g // 16, (g // 8) % 2, g % 8
                    sl = g % NPB
                    for c4 in range(4):
                        hh, ch = c4 // 2, c4 % 2
                        col, s0 = (2 * q + hh) * HD, 256 * half
                        tk = op("tensor", lambda e, c4=c4, hh=hh, ch=ch, col=col, t=t, j=j, sl=sl, s0=s0: e.matmul(
                            ps[32 * c4:32 * c4 + 32, 4 + j, s0:s0 + 256], vt[:, t, col:col + HD],
                            pr[:, sl, hh, ch * 512 + s0:ch * 512 + s0 + 256], start=(t == 0 and half == 0), stop=(t == 7),
                            skip_group_check=True),
                            [exp_tok[g], t_va] + (bank[4 + j] if t == 0 and half == 0 else []), tok=(c4 == 3))
                    if half == 0:
                        return
                    last_pv[0] = tk
                    p_free[sl].append(tk)
                    if t == 7:
                        post_half(b, q, j, tk, sum_tok[(q, j)])

                for g in range(16 * NP):
                    q, j, t = g // 16, (g // 8) % 2, g % 8
                    r = (b * NP + q) % RING
                    sl = g % NPB

                    def score(hh, r=r, j=j, t=t):
                        w = [t_ring[q], *(bank[2 * hh] + bank[2 * hh + 1])]
                        for c in range(2):
                            tk = op("tensor", lambda e, c=c: e.matmul(
                                ps[:, 2 * hh + c, :], kst[0:99, r, 2 * hh + j, t * 128:(t + 1) * 128],
                                qst[0:99, r, 2 * hh + j, c * 512:(c + 1) * 512], start=True, stop=True), w, tok=(c == 1))
                        return tk

                    def expo(hh, tk, sl=sl):
                        a = op("scalar", lambda e: e.activation(pr[:, sl, hh, :].rearrange("p (c n) -> p c n", c=2),
                               ps[:, 2 * hh:2 * hh + 2, :], ACT.Exp, scale=SCALE), [tk, *p_free[sl]], tok=True)
                        bank[2 * hh] = [a]
                        bank[2 * hh + 1] = [a]
                        return a

                    t0 = score(0)
                    if g >= LAG:
                        pv(g - LAG, 0)
                    tS = score(1)
                    if g >= LAG:
                        pv(g - LAG, 1)
                    filler()
                    expo(0, t0)
                    exp_tok[g] = expo(1, tS)
                    p_free[sl] = []
                    if t == 1:
                        d = op("vector", lambda e, j=j, s0=(g - 1) % NPB, s1=sl: e.tensor_tensor(
                            acc[:, j, :], pr[:, s0, :, :].rearrange("p a n -> p (a n)"),
                            pr[:, s1, :, :].rearrange("p a n -> p (a n)"), ALU.add), [exp_tok[g], *acc_free[j]], tok=True)
                        p_free[(g - 1) % NPB].append(d)
                        p_free[sl].append(d)
                        add_tok[0] = d
                    elif t > 1:
                        d = op("vector", lambda e, j=j, s1=sl: e.tensor_tensor(
                            acc[:, j, :], acc[:, j, :], pr[:, s1, :, :].rearrange("p a n -> p (a n)"), ALU.add),
                            [exp_tok[g], add_tok[0]], tok=True)
                        p_free[sl].append(d)
                        add_tok[0] = d
                    if t == 7:
                        sum_tok[(q, j)] = add_tok[0]
                    if g % 16 == 15:
                        ring_free[r] = [tS]
                        if q + RING < NP:
                            tl_[q + RING] = load_pair(b, q + RING, t_sc[(q + RING) // 2])
                    if g % 16 == 8 and q + 1 < NP:
                        t_ring[q + 1] = shift_pair(b, q + 1, t_zero, tl_[q + 1], [exp_tok[g]])
                    if b + 1 < B and g == 16:
                        for n, step in enumerate(prefetch_ln(b + 1, 0)):
                            at(2 * n + (2 if n > 4 else 0), step)
                    if b + 1 < B and 3 <= q < 7 and g % 16 == 10:
                        with_bank(6, lambda b6, k=q - 3: fill.append(lambda: turn(k, b6, ln_tok["ln"], True)))
                    tick()
                for i in range(LAG):
                    pv(16 * NP - LAG + i, 0)
                    pv(16 * NP - LAG + i, 1)
                dense[0] = True
                vt_free[:] = [last_pv[0]]
                d1_free = [last_pv[0], add_tok[0]]
            for i in range(2):
                magnitudes(i, [t_vp])
            while events or fill or urgent:
                tick()
            Q.fence([(s_x2, Q.value["s_x2"])])

        with ExitStack() as g2:
            with ExitStack() as al:
                zt = sbuf(al, "zt", [128, 2, 512], FR)
                zq = sbuf(al, "zq", [128, 512], FR)
                rb = sbuf(al, "rb", [128, 2, 512])
                sb2 = sbuf(al, "sb2", [128, 2, 512])
                hh_ = sbuf(al, "hh_", [128, 3, 512], FR)
                hl_ = sbuf(al, "hl_", [128, 3, 512], FR)
                fo = sbuf(al, "fo", [128, 4, E])
            sbuf(g2, "wf_place", [128, 3, HID])
            sbuf(g2, "ta_place", [128, 2, HID])
            tT = sbuf(g2, "tT", [128, 4, HID], FR)
            tP = sbuf(g2, "tP", [128, 16, E], FR)
            w2s = sbuf(g2, "w2s", [128, HID], FR)
            vth = sbuf(g2, "vth", [128, 4, 128], FR)
            vtl = sbuf(g2, "vtl", [128, 4, 128], FR)
            prow = sbuf(g2, "prow", [128, E])
            x2 = sbuf(g2, "x2", [128, 2, 4, E])
            xn = sbuf(g2, "xn", [128, 4, E])
            mv2 = sbuf(g2, "mv2", [128, 4, 2])
            st62 = sbuf(g2, "st62", [128, 4, 6])
            rs2 = sbuf(g2, "rs2", [128, 16])
            ln2 = sbuf(g2, "ln2", [128, 24])
            with ExitStack() as al:
                tt = sbuf(al, "tt", [128, 2, HID])
                us = sbuf(al, "us", [128, 16, RANK])
                ut = sbuf(al, "ut", [128, 2, 128])
                fba = sbuf(al, "fba", [128, 128])
                fbm = sbuf(al, "fbm", [128, 8, 128])
                vrep = sbuf(al, "vrep", [128, E])
                w2t = sbuf(al, "w2t", [128, 512], FR)
                dg = sbuf(al, "dg", [128, 4, 128])
                on1 = sbuf(al, "on1", [128, 128])
            with ExitStack() as al:
                yh = sbuf(al, "yh", [128, 2, 4, 512], FR)
                yl = sbuf(al, "yl", [128, 2, 4, 512], FR)

            s_u = Q.sem("s_u")
            s_fb = Q.sem("s_fb")
            s_x2l = [Q.sem("s_x2l0"), Q.sem("s_x2l1")]
            s_out = [Q.sem(f"s_out{o}") for o in range(4)]
            bank = {i: [] for i in range(8)}
            tt_free = [[], []]
            tr_n = [0]

            zb = [op("gpsimd", lambda e: e.memset(fba[:], 0.0), tok=True),
                  op("gpsimd", lambda e: e.memset(vrep[:], 0.0), tok=True),
                  op("gpsimd", lambda e: e.memset(on1[:], 1.0), tok=True)]
            t_u = dma("sync", s_u, us[:], u.rearrange("(t p) r -> p t r", p=128))
            x2_free, xn_free, x2tok, lntok = [[], []], [], {}, {}

            def load_rows(n):
                bf = n % 2
                x2tok[n] = dma("sync", s_x2l[bf], x2[:, bf, :, :],
                               x2d[n * 512:(n + 1) * 512, :].rearrange("(t p) e -> p t e", p=128), x2_free[bf])

            def norm_rows(n):
                return layernorm(x2[:, n % 2], xn, mv2, st62, rs2, ln2, 4, [x2tok[n]], lambda t: lntok.update({n: t}), xn_free)

            load_rows(0)
            load_rows(1)
            fb4 = fast_b.unsqueeze(1).broadcast_to([RANK, 4, RANK])
            for t8 in range(8):
                t_fb = dma("sync", s_fb, fba[16 * t8:16 * t8 + 16, :].rearrange("p (q c) -> p q c", q=4)[:, :, 0:16], fb4, zb)
            for q4 in range(4):
                t_fb = dma("sync", s_fb, vrep[32 * q4:32 * q4 + 16, :], v, zb)

            def ternary(i):
                fc, bf = i < 4, i % 2
                sc, c0, n = (scf, 4 * i, 4) if fc else (scp, i - 4, 1)
                cols = slice(c0, c0 + n)
                d = op("vector", lambda e: e.tensor_scalar(
                    sc[:, 0, cols], sc[:, 3, cols], 1.0 / (512 if fc else 2048), 1e-5, ALU.mult, ALU.max), [abs_tok[i]], tok=True)
                d1 = op("vector", lambda e: e.tensor_scalar(sc[:, 1, cols], sc[:, 0, cols], 0.5, None, ALU.mult), [d], tok=True)
                d2 = op("vector", lambda e: e.tensor_scalar(sc[:, 2, cols], sc[:, 0, cols], -0.5, None, ALU.mult), [d], tok=True)
                below = [op("vector", lambda e, col=col, c=c: e.tensor_scalar(
                    ta[:, bf, c], wf[:, i % 3, c], sc[:, 2, col:col + 1], None, ALU.is_lt), [d2, abs_tok[i]], tok=True)
                    for _, col, c in parts(i)]
                for (_, col, c), d3 in zip(parts(i), below):
                    d4 = op("vector", lambda e, col=col, c=c: e.scalar_tensor_tensor(
                        out=tt[:, bf, c], in0=wf[:, i % 3, c], scalar=sc[:, 1, col:col + 1], in1=ta[:, bf, c],
                        op0=ALU.is_gt, op1=ALU.subtract), [d1, d3, *tt_free[bf]], tok=True)
                ta_free[bf] = [d4]
                if i + 3 < 8:
                    load_weights(i + 3, [d4])
                if i + 2 < 8:
                    magnitudes(i + 2, [])
                for m in range(4):
                    bk = tr_n[0] % 8
                    tr_n[0] += 1
                    for k in range(4):
                        tk = op("tensor", lambda e, k=k, m=m, bk=bk: e.transpose(
                            ps[:, bk, k * 128:(k + 1) * 128], tt[:, bf, (4 * m + k) * 128:(4 * m + k + 1) * 128], ident[:]),
                            [d4, t_ident, *bank[bk]], tok=(k == 3))
                    if fc:
                        dst = tT[:, :, (4 * i + m) * 128:(4 * i + m + 1) * 128]
                    else:
                        dst = tP[:, 4 * m:4 * m + 4, (i - 4) * 128:(i - 3) * 128]
                    a = op("scalar", lambda e, dst=dst, bk=bk: e.activation(
                        dst, ps[:, bk, :].rearrange("p (k n) -> p k n", k=4), ACT.Copy), [tk], tok=True)
                    bank[bk] = [a]
                tt_free[bf] = [tk]
                return d4

            d_fc = None
            for i in range(4):
                d_fc = ternary(i)
            ternary(4)
            d = op("vector", lambda e: e.reciprocal(scf[:, 1, :], scf[:, 0, :]), [d_fc], tok=True)
            d = op("vector", lambda e: e.tensor_scalar(scf[:, 2, :], scf[:, 1, :], gatec, None, ALU.mult), [d, t_gate], tok=True)
            for t in range(16):
                t_us = op("vector", lambda e, t=t: e.tensor_scalar(us[:, t, :], us[:, t, :], scf[:, 2, t:t + 1], None,
                          ALU.mult), [d, t_u], tok=True)
            for t8 in range(8):
                t_fbm = op("vector", lambda e, t8=t8: e.tensor_scalar(fbm[:, t8, :], fba[:], ind[:, t8:t8 + 1], None,
                           ALU.mult), [t_fb, t_ind], tok=True)
            for g in range(2):
                tk = op("tensor", lambda e, g=g: e.transpose(ps[:, 1, g * 128:(g + 1) * 128],
                        us[:, 8 * g:8 * g + 8, :].rearrange("p t r -> p (t r)"), ident[:]), [t_us, *bank[1]], tok=True)
            t_ut = op("vector", lambda e: e.tensor_copy(ut[:].rearrange("p g n -> p (g n)"), ps[:, 1, 0:256]), [tk], tok=True)
            bank[1] = [t_ut]
            w2t_free = []
            for n in range(4):
                bk = 2 + n % 2
                for t in range(4):
                    i = 4 * n + t
                    tk = op("tensor", lambda e, i=i, t=t, bk=bk: e.matmul(ps[:, bk, t * 128:(t + 1) * 128], fbm[:, i % 8, :],
                            ut[:, i // 8, :], start=True, stop=True), [t_ut, t_fbm, *bank[bk]], tok=True)
                cols = slice(n * 512, (n + 1) * 512)
                a = op("scalar", lambda e, bk=bk: e.activation(w2t[:], ps[:, bk, :], ACT.Copy), [tk, *w2t_free], tok=True)
                wl = []
                for q4 in range(4):
                    rw = slice(32 * q4, 32 * q4 + 32)
                    if q4 % 2:
                        wl.append(op("vector", lambda e, rw=rw, cols=cols, bk=bk: e.tensor_tensor(
                            w2s[rw, cols], ps[rw, bk, :], w2t[rw, :], ALU.subtract), [a], tok=True))
                    else:
                        wl.append(op("vector", lambda e, rw=rw, cols=cols, bk=bk: e.tensor_copy(
                            w2s[rw, cols], ps[rw, bk, :]), [a], tok=True))
                bank[bk] = [a, wl[-1]]
                w2t_free = [wl[-1]]
            t_w2s = wl[-1]
            for k in range(4):
                tk = op("tensor", lambda e, k=k: e.transpose(ps[:, 4, k * 128:(k + 1) * 128], vrep[:, k * 128:(k + 1) * 128],
                        ident[:]), [t_fb, *bank[4]], tok=(k == 3))
            vsrc = ps[:, 4, :].rearrange("p (k n) -> p k n", k=4)
            a = op("scalar", lambda e: e.activation(vth[:], vsrc, ACT.Copy), [tk], tok=True)
            t_vt = op("vector", lambda e: e.tensor_tensor(vtl[:], vsrc, vth[:], ALU.subtract), [a], tok=True)
            bank[4] = [a, t_vt]
            for i in range(5, 8):
                d4 = ternary(i)
            for step in norm_rows(0):
                step()
            for n in range(4):
                d = op("vector", lambda e, n=n: e.tensor_scalar(dg[:, n, :], ident[:], scp[:, 0, n:n + 1], None, ALU.mult),
                       [d4], tok=True)
            tk = op("tensor", lambda e: e.matmul(ps[:, 0, :], on1[:], dg[:].rearrange("p a n -> p (a n)"), start=True,
                    stop=True), [d, *zb, *bank[0]], tok=True)
            t_prow = op("vector", lambda e: e.tensor_copy(prow[:], ps[:, 0, :]), [tk], tok=True)
            bank[0] = [t_prow]
            Q.fence()

            NB2 = B * S // 512
            bank = {i: [] for i in range(8)}
            y_free = [[], []]
            zt_free = [[], []]
            zq_free = []
            rb_free = [[], []]
            sb_free = [[], []]
            hid_free = [[], [], []]
            fo_free = [[], [], [], []]
            cnt = {"h": 0, "o": 0}
            ytok = {}
            ztok = {}

            def turn_rows(n, k):
                bf, bk = n % 2, 6 + k % 2
                for st in range(4):
                    tk = op("tensor", lambda e, st=st, k=k, bk=bk: e.transpose(
                        ps[:, bk, st * 128:(st + 1) * 128], xn[:, st, k * 128:(k + 1) * 128], ident[:]),
                        [lntok[n], *bank[bk]], tok=(st == 3))
                a = op("scalar", lambda e: e.activation(yh[:, bf, k, :], ps[:, bk, :], ACT.Copy), [tk, *y_free[bf]], tok=True)
                d = op("vector", lambda e: e.tensor_tensor(yl[:, bf, k, :], ps[:, bk, :], yh[:, bf, k, :], ALU.subtract),
                       [a, *y_free[bf]], tok=True)
                bank[bk] = [a, d]
                xn_free[:] = [tk]
                ytok[n] = d

            def low_rank(n):
                bf = n % 2
                i = 0
                for k in range(4):
                    for w_, y_ in ((vth, yh), (vtl, yh), (vth, yl)):
                        tk = op("tensor", lambda e, k=k, w_=w_, y_=y_, i=i: e.matmul(
                            ps[:, 6, :], w_[:, k, :], y_[:, bf, k, :], start=(i == 0), stop=(i == 11)),
                            [ytok[n], *bank[6]], tok=(i == 11))
                        i += 1
                a1 = op("scalar", lambda e: e.activation(zt[0:64, bf, :], ps[0:64, 6, :], ACT.Copy), [tk, *zt_free[bf]], tok=True)
                a2 = op("scalar", lambda e: e.activation(zq[64:128, :], ps[64:128, 6, :], ACT.Copy), [tk, *zq_free], tok=True)
                d = op("vector", lambda e: e.tensor_tensor(zt[64:128, bf, :], ps[64:128, 6, :], zq[64:128, :], ALU.subtract),
                       [a2, *zt_free[bf]], tok=True)
                zq_free[:] = [d]
                bank[6] = [a1, d]
                ztok[n] = [a1, d]

            def up(n, i):
                bf = n % 2
                h = cnt["h"]
                cnt["h"] += 1
                bk, r2, r3 = 4 + h % 2, h % 2, h % 3
                m = 0
                for k in range(4):
                    for y_ in (yh, yl):
                        op("tensor", lambda e, k=k, y_=y_, m=m: e.matmul(ps[:, bk, :], tT[:, k, i * 128:(i + 1) * 128],
                           y_[:, bf, k, :], start=(m == 0), stop=False), [ytok[n], *bank[bk]])
                        m += 1
                tk = op("tensor", lambda e: e.matmul(ps[:, bk, :], w2s[:, i * 128:(i + 1) * 128], zt[:, bf, :], start=False,
                        stop=True), ztok[n], tok=True)
                a = op("scalar", lambda e: e.activation(rb[:, r2, :], ps[:, bk, :], ACT.Relu, scale=scf[:, 0, i:i + 1]),
                       [tk, *rb_free[r2]], tok=True)
                bank[bk] = [a]
                d = op("vector", lambda e: e.tensor_tensor(sb2[:, r2, :], rb[:, r2, :], rb[:, r2, :], ALU.mult),
                       [a, *sb_free[r2]], tok=True)
                rb_free[r2] = [d]
                a = op("scalar", lambda e: e.activation(hh_[:, r3, :], sb2[:, r2, :], ACT.Copy), [d, *hid_free[r3]], tok=True)
                d = op("vector", lambda e: e.tensor_tensor(hl_[:, r3, :], sb2[:, r2, :], hh_[:, r3, :], ALU.subtract),
                       [a, d, *hid_free[r3]], tok=True)
                sb_free[r2] = [a, d]
                if i == 15:
                    y_free[bf] = [tk]
                    zt_free[bf] = [tk]
                return d, r3

            def down(n, i, hid):
                t_h, r3 = hid
                for rt in range(4):
                    for part, h_ in enumerate((hh_, hl_)):
                        tk = op("tensor", lambda e, rt=rt, h_=h_, part=part: e.matmul(
                            ps[:, rt, :], h_[:, r3, rt * 128:(rt + 1) * 128], tP[:, i, :],
                            start=(i == 0 and part == 0), stop=(i == 15 and part == 1)),
                            [t_h] + (bank[rt] if i == 0 else []), tok=(part == 1 and (rt == 3 or i == 15)))
                    if i == 15:
                        finish(n, rt, tk)
                hid_free[r3] = [tk]

            def finish(n, rt, tk):
                bf = n % 2
                o = rt
                d = op("vector", lambda e: e.tensor_tensor(fo[:, o, :], ps[:, rt, :], prow[:], ALU.mult), [tk, *fo_free[o]], tok=True)
                bank[rt] = [d]

                def residual():
                    t = op("vector", lambda e: e.tensor_tensor(fo[:, o, :], fo[:, o, :], x2[:, bf, rt, :], ALU.add),
                           [d], tok=True)
                    rows = n * 512 + rt * 128
                    fo_free[o] = [dma("sync", s_out[o], out_rows[rows:rows + 128, :], fo[:, o, :], [t])]
                    if rt == 3:
                        x2_free[bf] = [t]
                        if n + 2 < NB2:
                            load_rows(n + 2)
                later.append(residual)

            out_rows = out.rearrange("b s e -> (b s) e")
            for k in range(4):
                turn_rows(0, k)
            low_rank(0)
            prev = None
            later = []
            for n in range(NB2):
                for i in range(16):
                    hid = up(n, i)
                    if prev is not None:
                        down(*prev)
                    prev = (n, i, hid)
                    if i in (1, 2):
                        for fn in later[:2]:
                            fn()
                        del later[:2]
                    if n + 1 < NB2:
                        if i == 5:
                            steps = norm_rows(n + 1)
                        if i >= 5:
                            for step in steps[:3]:
                                step()
                            steps = steps[3:]
                        if 10 <= i < 14:
                            turn_rows(n + 1, i - 10)
                        if i == 14:
                            low_rank(n + 1)
            down(*prev)
            for fn in later:
                fn()
            op("sync", None, [f[0] for f in fo_free])

        with nc.Block() as block:
            Q.play(block)


_INS = ['L0_attn_x', 'L0_attn_w_qkv', 'L0_attn_wo', 'L0_attn_lambda_q1', 'L0_attn_lambda_q2', 'L0_attn_lambda_k1',
        'L0_attn_lambda_k2', 'L0_attn_norm_w', 'L0_ffn_fast_b', 'L0_ffn_w_fc', 'L0_ffn_w_proj', 'L0_ffn_u', 'L0_ffn_v',
        'L0_ffn_gate']
_OUTS = [((B, S, E), 'float32')]


def kernel(**inputs):
    import numpy as _np
    import concourse.bacc as _bacc
    from concourse import mybir as _mybir
    from concourse.bass_utils import run_bass_kernel_spmd as _run

    nc = _bacc.Bacc("TRN2", target_bir_lowering=False, num_devices=1)
    arrays, args = {}, []
    for name in _INS:
        a = _np.ascontiguousarray(inputs[name])
        arrays[f"in_{name}_dram"] = a
        args.append(nc.dram_tensor(f"in_{name}_dram", a.shape, _mybir.dt.from_np(a.dtype), kind="ExternalInput").ap())
    for i, (shape, dtype) in enumerate(_OUTS):
        dt = _mybir.dt.from_np(_np.dtype(dtype))
        args.append(nc.dram_tensor(f"out_{i}_dram", shape, dt, kind="ExternalOutput").ap())
    build(nc, *args)
    r = _run(nc, [arrays], core_ids=[0])
    got = tuple(r.results[0][f"out_{i}_dram"] for i in range(len(_OUTS)))
    return got[0]
```
